# Optimizing a Trainium2 kernel written in Bass

```python
import numpy as np
import jax
import jax.numpy as jnp

def _softmax(x, axis=-1):
    return jax.nn.softmax(x, axis=axis)

def _gelu(x):
    return jax.nn.gelu(x, approximate=True)

def _silu(x):
    return jax.nn.silu(x)

def _sigmoid(x):
    return jax.nn.sigmoid(x)

def _layernorm(x, axis=-1, eps=1e-05):
    m = jnp.mean(x, axis=axis, keepdims=True)
    v = jnp.var(x, axis=axis, keepdims=True)
    return (x - m) / jnp.sqrt(v + eps)

def _scatter_add(tgt, idx, src, axis=0):
    return tgt.at[idx].add(src)

def _segment_sum(src, seg, n):
    return jax.ops.segment_sum(src, seg, n)
kernel_name = 'mk_seq_preln_d1_jaxref_r4_8678d0'

def setup_inputs(seed: int=0):
    np.random.seed(seed)
    _w = jnp.asarray

    def _L0_attn_setup():
        import math
        import jax, jax.numpy as jnp
        import numpy as np
        N_HEADS = 8
        EPS = 1e-05
        key = jax.random.key(seed)
        ks = jax.random.split(key, 5)
        B, L, D = (4, 512, 256)
        w_scale = 0.02
        return {'x': jax.random.normal(ks[0], (B, L, D), dtype=jnp.float32), 'Wq': jax.random.normal(ks[1], (D, D), dtype=jnp.float32) * w_scale, 'Wk': jax.random.normal(ks[2], (D, D), dtype=jnp.float32) * w_scale, 'Wv': jax.random.normal(ks[3], (D, D), dtype=jnp.float32) * w_scale, 'Wo': jax.random.normal(ks[4], (D, D), dtype=jnp.float32) * w_scale, 'gn_weight': jnp.ones((D,), dtype=jnp.float32), 'gn_bias': jnp.zeros((D,), dtype=jnp.float32)}
    _L0_attn_in = _L0_attn_setup()

    def _L0_ffn_setup():
        import jax, jax.numpy as jnp
        import numpy as np
        MAX_VAL = 100.0
        key = jax.random.key(seed)
        k1, k2, k3 = jax.random.split(key, 3)
        B, S, D_IN, D_OUT = (4, 2048, 256, 256)
        x = jax.random.normal(k1, (B, S, D_IN), dtype=jnp.float32)
        weights = jax.random.normal(k2, (D_OUT, D_IN), dtype=jnp.float32)
        scale = jnp.ones((D_OUT,), dtype=jnp.float32)
        bias = jax.random.normal(k3, (D_OUT,), dtype=jnp.float32)
        return {'x': x, 'weights': weights, 'scale': scale, 'bias': bias}
    _L0_ffn_in = _L0_ffn_setup()
    _d = {'L0_attn_x': _L0_attn_in['x'], 'L0_attn_Wq': _L0_attn_in['Wq'], 'L0_attn_Wk': _L0_attn_in['Wk'], 'L0_attn_Wv': _L0_attn_in['Wv'], 'L0_attn_Wo': _L0_attn_in['Wo'], 'L0_attn_gn_weight': _L0_attn_in['gn_weight'], 'L0_attn_gn_bias': _L0_attn_in['gn_bias'], 'L0_ffn_weights': _L0_ffn_in['weights'], 'L0_ffn_scale': _L0_ffn_in['scale'], 'L0_ffn_bias': _L0_ffn_in['bias']}
    _x0 = _d['L0_attn_x']
    _d['L0_attn_x'] = jax.random.normal(jax.random.fold_in(jax.random.key(seed), 1), (8, 512, 256), dtype=_x0.dtype)
    del _x0
    return _d

def reference(L0_attn_x, L0_attn_Wq, L0_attn_Wk, L0_attn_Wv, L0_attn_Wo, L0_attn_gn_weight, L0_attn_gn_bias, L0_ffn_weights, L0_ffn_scale, L0_ffn_bias):

    def _L0_attn_ref(x, Wq, Wk, Wv, Wo, gn_weight, gn_bias):
        import math
        import jax, jax.numpy as jnp
        import numpy as np
        N_HEADS = 8
        EPS = 1e-05
        B, L, D = x.shape
        H = N_HEADS
        dh = D // H
        gammas = 1.0 - jnp.exp(jnp.linspace(math.log(1.0 / 32.0), math.log(1.0 / 512.0), H)).astype(x.dtype)

        def proj(W):
            return (x @ W.T).reshape(B, L, H, dh).transpose(1, 0, 2, 3)
        qT, kT, vT = (proj(Wq), proj(Wk), proj(Wv))
        g = gammas[None, :, None, None]

        def step(S, qkv_t):
            q_t, k_t, v_t = qkv_t
            S = g * S + k_t[..., :, None] * v_t[..., None, :]
            y_t = jnp.einsum('bhde,bhd->bhe', S, q_t)
            return (S, y_t)
        S0 = jnp.zeros((B, H, dh, dh), dtype=x.dtype)
        _, ys = jax.lax.scan(step, S0, (qT, kT, vT))
        out = ys.transpose(1, 0, 2, 3)
        mean = out.mean(axis=(1, 3), keepdims=True)
        var = out.var(axis=(1, 3), keepdims=True)
        out = (out - mean) * jax.lax.rsqrt(var + EPS)
        out = out.reshape(B, L, D) * gn_weight + gn_bias
        return out @ Wo.T

    def _L0_ffn_ref(x, weights, scale, bias):
        import jax, jax.numpy as jnp
        import numpy as np
        MAX_VAL = 100.0
        w = (weights >= 0.0).astype(x.dtype) * 2.0 - 1.0
        y = jnp.einsum('bsi,oi->bso', x, w)
        y = y * scale + bias
        y = jnp.clip(y, -MAX_VAL, MAX_VAL)
        return y
    x = L0_attn_x
    x = x + _L0_attn_ref(_layernorm(x, axis=-1), L0_attn_Wq, L0_attn_Wk, L0_attn_Wv, L0_attn_Wo, L0_attn_gn_weight, L0_attn_gn_bias)
    x = x + _L0_ffn_ref(_layernorm(x, axis=-1), L0_ffn_weights, L0_ffn_scale, L0_ffn_bias)
    return x

_drawn_inputs = setup_inputs


def setup_inputs(seed=0):
    import zlib

    import numpy as np

    out = dict(_drawn_inputs(seed))
    spreads = {'L0_attn_gn_weight': (1.0, 0.2),
     'L0_attn_gn_bias': (0.0, 0.298),
     'L0_ffn_scale': (1.0, 0.2)}
    factors = {}
    for name, (base, spread) in spreads.items():
        noise = np.random.default_rng([zlib.crc32(name.encode()), seed]).standard_normal(out[name].shape)
        drawn = base * np.exp(spread * noise) if base else spread * noise
        out[name] = jnp.asarray(drawn.astype(out[name].dtype))
    for name, factor in factors.items():
        out[name] = (out[name] * factor).astype(out[name].dtype)
    return out
```

```python
from contextlib import ExitStack

import numpy as np

import concourse.bass as bass
from concourse import mybir

F32 = mybir.dt.float32
F16 = mybir.dt.float16
ALU = mybir.AluOpType
ACT = mybir.ActivationFunctionType

P = 128
B = 8
L = 512
D = 256
H = 8
DH = D // H
KC = D // P
HG = P // DH
NT = L // P
EPS = 1e-5
MAX_VAL = 100.0


class Seq:

    def __init__(self, offset, turn=None):
        self.offset, self.turn = offset, turn
        self.parity = offset % 2

    def __add__(self, k):
        return Seq(self.offset + k, self.turn)

    def count(self, each, more=0):
        fixed = self.offset * each + more
        return fixed if self.turn is None else self.turn * (2 * each) + fixed

    def same_parity_count(self, each, more=0):
        fixed = self.offset // 2 * each + more
        return fixed if self.turn is None else self.turn * each + fixed

    def is_(self, n):
        return self.turn is None and self.offset == n


def build(nc, x, wq_t, wk_t, wv_t, wo_t, ffn_t, columns, decay_q, decay_k, squares, out):
    x_v = x.rearrange("b (j p) c -> b p j c", p=P)
    out_v = out.rearrange("b (j p) c -> b p j c", p=P)
    halves = lambda w: w.rearrange("(k p) n -> p k n", p=P)

    with ExitStack() as ctx:
        def sb(name, shape, dt=F32):
            return ctx.enter_context(nc.sbuf_tensor(name, shape, dt))

        def sem(name):
            return ctx.enter_context(nc.semaphore(name))

        wq = sb("wq", [P, KC, D])
        wk = sb("wk", [P, KC, D])
        wv = sb("wv", [P, KC, D])
        wo = sb("wo", [P, KC, D])
        wf = sb("wf", [P, KC, D])
        wpos = sb("wpos", [P, KC, D])
        wsign = sb("wsign", [P, KC, D], F16)
        cols = sb("cols", [P, 4, KC])
        dq = sb("dq", [P, KC, L])
        dk = sb("dk", [P, KC, L])
        sq = sb("sq", [P, 4, P])
        ident, causal, same_head, head_avg = (sq[:, n, :] for n in range(4))
        neg_half = sb("neg_half", [P, NT])
        dve_gate, pool_gate = sb("dve_gate", [P, 1]), sb("pool_gate", [P, 1])

        xs = [sb(f"xs{p}", [P, NT, D]) for p in range(2)]
        st1 = sb("st1", [P, NT, 6])
        mv1 = sb("mv1", [P, NT, 2])
        nm1 = sb("nm1", [P, NT])
        ve1 = sb("ve1", [P, NT])
        rs1 = sb("rs1", [P, NT])
        xn = sb("xn", [P, NT, D])
        xnT = sb("xnT", [P, KC, L])
        qT = sb("qT", [P, KC, L])
        kT = sb("kT", [P, KC, L])
        ktok = sb("ktok", [P, NT, D])
        v = sb("v", [P, NT, D])
        probs = [sb(f"probs{p}", [P, HG, P]) for p in range(2)]
        state = [sb(f"state{p}", [P, KC, P]) for p in range(2)]
        gst = sb("gst", [P, KC, 6])
        gmv = sb("gmv", [P, KC, 2])
        gmean = sb("gmean", [P, KC])
        gdev = sb("gdev", [P, KC])
        gdev2 = sb("gdev2", [P, KC])
        gz = sb("gz", [P, KC])
        gve = sb("gve", [P, KC])
        grs = sb("grs", [P, KC])
        gscale = sb("gscale", [P, KC])
        gms = sb("gms", [P, KC])
        gbias = sb("gbias", [P, KC])
        yn = sb("yn", [P, KC, L])
        x1 = [sb(f"x1_{p}", [P, NT, D]) for p in range(2)]
        st2 = sb("st2", [P, NT, 6])
        mv2 = sb("mv2", [P, NT, 2])
        nm2 = sb("nm2", [P, NT])
        ve2 = sb("ve2", [P, NT])
        rs2 = sb("rs2", [P, NT])
        xn2 = sb("xn2", [P, NT, D])
        hi = sb("hi", [P, KC, L], F16)
        lo = sb("lo", [P, KC, L], F16)
        fT = sb("fT", [P, KC, L])
        clipped = sb("clipped", [P, NT, D])
        res = [sb(f"res{p}", [P, NT, D]) for p in range(2)]

        ps = ctx.enter_context(nc.psum_tensor("ps", [P, 8, 512], F32))
        Y, STATE, MISC = 4, 6, 7

        w_in = sem("w_in")
        x_in = [sem(f"x_in{p}") for p in range(2)]
        stored = [sem(f"stored{p}") for p in range(2)]
        sign_step = sem("sign_step")
        xnT_ps, q_ps, k_ps, v_ps = sem("xnT_ps"), sem("q_ps"), sem("k_ps"), sem("v_ps")
        gn_ps, wo_ps, ktok_ps = sem("gn_ps"), sem("wo_ps"), sem("ktok_ps")
        scores_ps = sem("scores_ps")
        state_ps = sem("state_ps")
        y_ps = sem("y_ps")
        xn2T_ps, ffn_ps, back_ps = sem("xn2T_ps"), sem("ffn_ps"), sem("back_ps")
        aggr1, ln1_st = sem("aggr1"), sem("ln1_st")
        q_sb, k_sb = sem("q_sb"), sem("k_sb")
        gn_st = sem("gn_st")
        x1_sb = sem("x1_sb")
        aggr2, ln2_st = sem("aggr2"), sem("ln2_st")
        masked = sem("masked")
        state_sb = sem("state_sb")
        lo_sb, clip_sb = sem("lo_sb"), sem("clip_sb")
        xnT_sb, v_sb, yn_sb, ktok_sb = sem("xnT_sb"), sem("v_sb"), sem("yn_sb"), sem("ktok_sb")
        hi_sb, fT_sb = sem("hi_sb"), sem("fT_sb")
        const_ok, x_copied = sem("const_ok"), sem("x_copied")
        rs1_ok, xn_ok, grs_ok, rs2_ok, xn2_ok, res_ok = (
            sem(n) for n in ("rs1_ok", "xn_ok", "grs_ok", "rs2_ok", "xn2_ok", "res_ok"))

        UNITS = NT * KC
        GN_STEPS = 13
        FREE = 1
        N_W = 9 * 16

        def steps(eng, step):
            step(Seq(0), True)
            with eng.Fori(0, (B - 2) // 2) as r:
                odd = Seq(1, r)
                step(odd, True)
                step(odd + 1, True)
            step(Seq(B - 1), True, last=True)
            step(Seq(B), False, last=True)

        block = ctx.enter_context(nc.Block())

        @block.sync
        def _(sp):
            def load_x(s):
                if not s.is_(1):
                    sp.wait_ge(x_copied, (s + -1).count(1))
                sp.dma_start(xs[s.parity][:, :, :], x_v[s.count(1)]).then_inc(x_in[s.parity], 16)

            sp.dma_start(xs[0][:, :, :], x_v[0]).then_inc(x_in[0], 16)
            for sbuf, dram in ((sq, squares.rearrange("n p m -> p n m")), (wq, halves(wq_t)),
                               (dq, halves(decay_q)), (wk, halves(wk_t)), (dk, halves(decay_k)),
                               (wv, halves(wv_t)),
                               (cols, columns)):
                sp.dma_start(sbuf[:, :, :], dram).then_inc(w_in, 16)
            sp.dma_start(xs[1][:, :, :], x_v[1]).then_inc(x_in[1], 16)
            for sbuf, dram in ((wo, halves(wo_t)), (wf, halves(ffn_t))):
                sp.dma_start(sbuf[:, :, :], dram).then_inc(w_in, 16)

            def step(cur, has_cur, last=False):
                is_first = cur.is_(0)
                if is_first:
                    return
                prev = cur + -1
                if not last:
                    load_x(cur + 1)
                sp.wait_ge(res_ok, prev.count(1, 1 + FREE))
                sp.dma_start(out_v[prev.count(1)], res[prev.parity][:, :, :]).then_inc(stored[prev.parity], 16)

            steps(sp, step)
            for p in range(2):
                sp.wait_ge(stored[p], 16 * (B // 2) + FREE)

        @block.tensor
        def _(pe):
            def xn_transposes(s, kc):
                if kc == 0:
                    pe.wait_ge(xn_ok, s.count(1, 1))
                for j in range(NT):
                    mm = pe.transpose(ps[:, MISC, j * P:(j + 1) * P], xn[:, j, kc * P:(kc + 1) * P], ident)
                mm.then_inc(xnT_ps, 1)

            def project_qk(s, w, bank, done):
                for g in range(KC):
                    for kc in range(KC):
                        mm = pe.matmul(ps[:, bank + g, :], w[:, kc, g * P:(g + 1) * P], xnT[:, kc, :],
                                       start=(kc == 0), stop=(kc == KC - 1))
                    mm.then_inc(done, 1)
                    yield

            def project_v(s, half):
                bank = (MISC, STATE)[half]
                for j in range(2):
                    for kc in range(KC):
                        t = 2 * half + j
                        mm = pe.matmul(ps[:, bank, j * D:(j + 1) * D], xnT[:, kc, t * P:(t + 1) * P],
                                       wv[:, kc, :], start=(kc == 0), stop=(kc == KC - 1))
                mm.then_inc(v_ps, 1)

            def out_projection(s, half):
                for j in range(2):
                    t = 2 * half + j
                    for kc in range(KC):
                        mm = pe.matmul(ps[:, half, j * D:(j + 1) * D], yn[:, kc, t * P:(t + 1) * P],
                                       wo[:, kc, :], start=(kc == 0), stop=(kc == KC - 1))
                mm.then_inc(wo_ps, 1)

            def k_transposes(s, half):
                for j in range(2):
                    c = 2 * half + j
                    for g in range(KC):
                        mm = pe.transpose(ps[:, 2 + half, j * D + g * P:j * D + (g + 1) * P],
                                          kT[:, g, c * P:(c + 1) * P], ident)
                mm.then_inc(ktok_ps, 1)

            def scores(s, u):
                c, g = divmod(u, KC)
                for h in range(HG):
                    rows = slice(h * DH, (h + 1) * DH)
                    mm = pe.matmul(ps[:, h, 0:P], kT[rows, g, c * P:(c + 1) * P], qT[rows, g, c * P:(c + 1) * P],
                                   start=True, stop=True)
                mm.then_inc(scores_ps, 1)

            def update_state(s, c):
                if c == 0:
                    pe.wait_ge(v_sb, s.count(2, 2))
                else:
                    pe.wait_ge(state_sb, s.count(3, c))
                for g in range(KC):
                    mm = pe.matmul(ps[:, STATE, g * P:(g + 1) * P], ktok[:, c, g * P:(g + 1) * P],
                                   v[:, c, g * P:(g + 1) * P], start=(c == 0 and g == 0), stop=(c == NT - 2),
                                   skip_group_check=True)
                mm.then_inc(state_ps, 1)

            def outputs(s, u):
                c, g = divmod(u, KC)
                ys = ps[:, Y + g, c * P:(c + 1) * P]
                if c:
                    if g == 0:
                        pe.wait_ge(state_sb, s.count(3, c))
                    pe.matmul(ys, state[(c - 1) % 2][:, g, :], qT[:, g, c * P:(c + 1) * P],
                              start=True, stop=False, skip_group_check=True)
                for h in range(HG):
                    mm = pe.matmul(ps[h * DH:(h + 1) * DH, Y + g, c * P:(c + 1) * P],
                                   v[:, c, g * P + h * DH:g * P + (h + 1) * DH], probs[u % 2][:, h, :],
                                   start=(c == 0), stop=True, skip_group_check=True)
                if u == UNITS - 1:
                    mm.then_inc(y_ps, 1)

            def xn2_transposes(s, kc):
                if kc == 0:
                    pe.wait_ge(xn2_ok, s.count(1, 1 + FREE))
                for j in range(NT):
                    mm = pe.transpose(ps[:, MISC, j * P:(j + 1) * P], xn2[:, j, kc * P:(kc + 1) * P], ident)
                mm.then_inc(xn2T_ps, 1)

            def ffn(s, o):
                n = 0
                for part in (hi, lo):
                    for kc in range(KC):
                        mm = pe.matmul(ps[:, MISC, :], wsign[:, kc, o * P:(o + 1) * P], part[:, kc, :],
                                       start=(n == 0), stop=(n == 2 * KC - 1))
                        n += 1
                mm.then_inc(ffn_ps, 1)

            def back_transposes(s, half):
                for j in range(2):
                    t = 2 * half + j
                    for o in range(KC):
                        mm = pe.transpose(ps[:, MISC, j * D + o * P:j * D + (o + 1) * P],
                                          fT[:, o, t * P:(t + 1) * P], ident)
                mm.then_inc(back_ps, 1)

            def misc(n, cur, has_cur, last):
                prev = cur + -1
                has_prev = not (cur.is_(0))
                if n < 2 and not last:
                    nxt = cur + 1
                    if n == 0:
                        pe.wait_ge(v_sb, cur.count(2, 1))
                    else:
                        pe.wait_ge(xnT_sb, nxt.count(2, 1))
                    xn_transposes(nxt, n)
                if not has_prev:
                    return
                if n == 2:
                    if not last:
                        pe.wait_ge(xnT_sb, cur.count(2, 4))
                    elif has_cur:
                        pe.wait_ge(v_sb, cur.count(2, 1))
                    xn2_transposes(prev, 0)
                if n == 3:
                    pe.wait_ge(lo_sb, prev.count(2, 1))
                    xn2_transposes(prev, 1)
                if n == 4:
                    pe.wait_ge(lo_sb, prev.count(2, 2))
                    ffn(prev, 0)
                if n == 5:
                    pe.wait_ge(fT_sb, prev.count(2, 1))
                    ffn(prev, 1)
                if n == 6:
                    pe.wait_ge(fT_sb, prev.count(2, 2))
                    back_transposes(prev, 0)
                if n == 7:
                    pe.wait_ge(clip_sb, prev.count(2, 1 + FREE))
                    back_transposes(prev, 1)

            def step(cur, has_cur, last=False):
                has_prev = not (cur.is_(0))
                prev = cur + -1
                if has_cur:
                    pe.wait_ge(xnT_sb, cur.count(2, 2))
                    if has_prev:
                        pe.wait_ge(masked, cur.count(UNITS))
                    q = project_qk(cur, wq, 0, q_ps)
                    k = project_qk(cur, wk, 2, k_ps)
                    next(q)
                    next(q)
                if has_prev:
                    pe.wait_ge(gn_st, prev.count(GN_STEPS, 4))
                    if not (cur.is_(1)):
                        pe.wait_ge(clip_sb, prev.count(2, FREE))
                    pe.matmul(ps[:, MISC, 0:KC], head_avg, gmv[:, :, 0], start=True, stop=True).then_inc(gn_ps, 1)
                if has_cur:
                    next(k)
                if has_prev:
                    pe.wait_ge(gn_st, prev.count(GN_STEPS, 8))
                    pe.matmul(ps[:, MISC, 0:KC], head_avg, gz[:, :], start=True, stop=True).then_inc(gn_ps, 1)
                if has_cur:
                    next(k)
                    if has_prev:
                        pe.wait_ge(gn_st, prev.count(GN_STEPS, 9))
                    project_v(cur, 0)
                    if has_prev:
                        pe.wait_ge(state_sb, cur.count(3))
                    project_v(cur, 1)
                if has_prev:
                    for half in range(2):
                        pe.wait_ge(yn_sb, prev.count(2, 2))
                        if has_cur:
                            pe.wait_ge(q_sb, cur.count(2, 1 + half))
                        else:
                            pe.wait_ge(masked, prev.count(UNITS, UNITS))
                        out_projection(prev, half)
                if has_cur:
                    pe.wait_ge(k_sb, cur.count(2, 2))
                    for half in range(2):
                        k_transposes(cur, half)
                    pe.wait_ge(ktok_sb, cur.count(2, 2))
                    if has_prev:
                        pe.wait_ge(x1_sb, prev.count(2, 2))
                    else:
                        pe.wait_ge(q_sb, 2)
                    scores(cur, 0)
                    for u in range(UNITS):
                        c, g = divmod(u, KC)
                        if g == 0 and c < NT - 1:
                            update_state(cur, c)
                        misc(u, cur, has_cur, last)
                        pe.wait_ge(masked, cur.count(UNITS, u + 1))
                        if u + 1 < UNITS:
                            scores(cur, u + 1)
                        outputs(cur, u)
                else:
                    for n in range(2, 8):
                        misc(n, cur, has_cur, last)

            pe.wait_ge(w_in, N_W)
            xn_transposes(Seq(0), 0)
            pe.wait_ge(xnT_sb, 1)
            xn_transposes(Seq(0), 1)
            pe.wait_ge(sign_step, 2)
            steps(pe, step)

        @block.vector
        def _(dve):
            def ln_stats(s, src, st, mv, nm, ve, aggr, done, seen, count):
                for j in range(NT):
                    if j < 1:
                        seen()
                    if j == 2 and seen is not None and count:
                        dve.wait_ge(*count)
                    dve.bn_stats(st[:, j, :], src[:, j, :]).then_inc(aggr, 1)
                dve.wait_ge(aggr, s.count(2 * NT, NT))
                dve.memset(dve_gate[:, :], 0.0)
                for j in range(NT):
                    dve.bn_aggr(mv[:, j, :], st[:, j, :]).then_inc(aggr, 1)
                dve.wait_ge(aggr, s.count(2 * NT, 2 * NT))
                dve.tensor_scalar(nm[:, :], mv[:, :, 0], -1.0, None, ALU.mult).then_inc(done, 1)
                dve.tensor_scalar(ve[:, :], mv[:, :, 1], EPS, None, ALU.add).then_inc(done, 1)

            def ln1(s):
                def seen():
                    dve.wait_ge(x_in[s.parity], s.same_parity_count(16, 16))
                    if not (s.is_(0)):
                        dve.wait_ge(xn_ok, s.count(1))
                ln_stats(s, xs[s.parity], st1, mv1, nm1, ve1, aggr1, ln1_st, seen, None)

            def ln2(s):
                def seen():
                    dve.wait_ge(x1_sb, s.count(2, 2))
                    if not (s.is_(0)):
                        dve.wait_ge(xn2_ok, s.count(1, FREE))
                ln_stats(s, x1[s.parity], st2, mv2, nm2, ve2, aggr2, ln2_st, seen, None)

            def decayed(s, g, bank, seen, table, dst, done):
                dve.wait_ge(seen, s.count(2, g + 1))
                dve.tensor_tensor(dst[:, g, :], ps[:, bank + g, :], table[:, g, :], ALU.mult).then_inc(done, 1)

            def gn_rows(s):
                dve.wait_ge(y_ps, s.count(1, 1))
                for g in range(KC):
                    dve.bn_stats(gst[:, g, :], ps[:, Y + g, :]).then_inc(gn_st, 1)
                dve.wait_ge(gn_st, s.count(GN_STEPS, 2))
                dve.memset(dve_gate[:, :], 0.0)
                for g in range(KC):
                    dve.bn_aggr(gmv[:, g, :], gst[:, g, :]).then_inc(gn_st, 1)

            def gn_deviation(s):
                dve.wait_ge(gn_ps, s.count(2, 1))
                dve.wait_ge(gn_st, s.count(GN_STEPS, 4))
                dve.tensor_copy(gmean[:, :], ps[:, MISC, 0:KC]).then_inc(gn_st, 1)
                dve.wait_ge(gn_st, s.count(GN_STEPS, 5))
                dve.tensor_tensor(gdev[:, :], gmv[:, :, 0], gmean[:, :], ALU.subtract).then_inc(gn_st, 1)
                dve.wait_ge(gn_st, s.count(GN_STEPS, 6))
                dve.tensor_tensor(gdev2[:, :], gdev[:, :], gdev[:, :], ALU.mult).then_inc(gn_st, 1)
                dve.wait_ge(gn_st, s.count(GN_STEPS, 7))
                dve.tensor_tensor(gz[:, :], gdev2[:, :], gmv[:, :, 1], ALU.add).then_inc(gn_st, 1)

            def gn_variance(s):
                dve.wait_ge(gn_ps, s.count(2, 2))
                dve.tensor_scalar(gve[:, :], ps[:, MISC, 0:KC], EPS, None, ALU.add).then_inc(gn_st, 1)

            def gn_affine(s):
                dve.wait_ge(grs_ok, s.count(1, 1))
                dve.tensor_tensor(gscale[:, :], grs[:, :], cols[:, 0, :], ALU.mult).then_inc(gn_st, 1)
                dve.wait_ge(gn_st, s.count(GN_STEPS, 10))
                dve.tensor_tensor(gms[:, :], gmean[:, :], gscale[:, :], ALU.mult).then_inc(gn_st, 1)
                dve.wait_ge(gn_st, s.count(GN_STEPS, 11))
                dve.tensor_tensor(gbias[:, :], cols[:, 1, :], gms[:, :], ALU.subtract).then_inc(gn_st, 2)

            def residual(s, half):
                dve.wait_ge(wo_ps, s.count(2, half + 1))
                if half == 0:
                    dve.wait_ge(x_copied, s.count(1, 1))
                j = slice(2 * half, 2 * half + 2)
                dve.tensor_tensor(x1[s.parity][:, j, :], ps[:, half, :].rearrange("p (j c) -> p j c", j=2),
                                  x1[s.parity][:, j, :], ALU.add).then_inc(x1_sb, 1)

            def mask(s, u):
                dve.wait_ge(scores_ps, s.count(UNITS, u + 1))
                dve.tensor_tensor(probs[u % 2][:, :, :], ps[:, 0:HG, 0:P],
                                  causal.rearrange("p (a t) -> p a t", a=1).broadcast_to([P, HG, P]),
                                  ALU.mult).then_inc(masked, 1)

            def copy_state(s, c):
                dve.wait_ge(state_ps, s.count(3, c + 1))
                dve.tensor_tensor(state[c % 2][:, :, :], ps[:, STATE, 0:KC * P].rearrange("p (g n) -> p g n", g=KC),
                                  same_head.rearrange("p (a t) -> p a t", a=1).broadcast_to([P, KC, P]),
                                  ALU.mult).then_inc(state_sb, 1)

            def low_part(s, kc):
                dve.wait_ge(hi_sb, s.count(2, kc + 1))
                dve.tensor_tensor(lo[:, kc, :], ps[:, MISC, :], hi[:, kc, :], ALU.subtract).then_inc(lo_sb, 1)

            def clip(s, half):
                dve.wait_ge(back_ps, s.count(2, half + 1))
                if half == 0 and not (s.is_(0)):
                    dve.wait_ge(res_ok, s.count(1, FREE))
                dve.tensor_scalar(clipped[:, 2 * half:2 * half + 2, :],
                                  ps[:, MISC, :].rearrange("p (j c) -> p j c", j=2),
                                  MAX_VAL, -MAX_VAL, ALU.min, ALU.max).then_inc(clip_sb, 1)

            def step(cur, has_cur, last=False):
                has_prev = not (cur.is_(0))
                prev = cur + -1
                if has_prev:
                    gn_rows(prev)
                if has_cur:
                    for g in range(KC):
                        decayed(cur, g, 0, q_ps, dq, qT, q_sb)
                if has_prev:
                    gn_deviation(prev)
                if has_cur:
                    decayed(cur, 0, 2, k_ps, dk, kT, k_sb)
                if has_prev:
                    gn_variance(prev)
                if has_cur:
                    decayed(cur, 1, 2, k_ps, dk, kT, k_sb)
                if has_prev:
                    gn_affine(prev)
                if not last:
                    ln1(cur + 1)
                if has_prev:
                    residual(prev, 0)
                    residual(prev, 1)
                if has_cur:
                    for u in range(UNITS):
                        c, g = divmod(u, KC)
                        mask(cur, u)
                        if g == 0 and c < NT - 1:
                            copy_state(cur, c)
                        if has_prev:
                            if u == 0:
                                ln2(prev)
                            if u in (2, 3):
                                low_part(prev, u - 2)
                            if u in (6, 7):
                                clip(prev, u - 6)
                else:
                    ln2(prev)
                    low_part(prev, 0)
                    low_part(prev, 1)
                    clip(prev, 0)
                    clip(prev, 1)

            ln1(Seq(0))
            dve.wait_ge(w_in, N_W)
            dve.tensor_scalar(wpos[:, :, :], wf[:, :, :], 0.0, 2.0, ALU.is_ge, ALU.mult).then_inc(sign_step, 1)
            dve.wait_ge(sign_step, 1)
            dve.tensor_scalar(wsign[:, :, :], wpos[:, :, :], -1.0, None, ALU.add).then_inc(sign_step, 1)
            steps(dve, step)

        @block.scalar
        def _(act):
            def copy_xnT(s, kc):
                act.wait_ge(xnT_ps, s.count(2, kc + 1))
                act.copy(xnT[:, kc, :], ps[:, MISC, :]).then_inc(xnT_sb, 1)

            def step(cur, has_cur, last=False):
                has_prev = not (cur.is_(0))
                prev = cur + -1
                if has_cur:
                    for half in range(2):
                        act.wait_ge(v_ps, cur.count(2, half + 1))
                        act.copy(v[:, 2 * half:2 * half + 2, :],
                                 ps[:, (MISC, STATE)[half], :].rearrange("p (j c) -> p j c", j=2)).then_inc(v_sb, 1)
                if has_prev:
                    act.wait_ge(gn_st, prev.count(GN_STEPS, GN_STEPS))
                    for g in range(KC):
                        act.activation(yn[:, g, :], ps[:, Y + g, :], ACT.Identity, bias=gbias[:, g:g + 1],
                                       scale=gscale[:, g:g + 1]).then_inc(yn_sb, 1)
                if has_cur:
                    for half in range(2):
                        act.wait_ge(ktok_ps, cur.count(2, half + 1))
                        act.copy(ktok[:, 2 * half:2 * half + 2, :],
                                 ps[:, 2 + half, :].rearrange("p (j c) -> p j c", j=2)).then_inc(ktok_sb, 1)
                if not last:
                    for kc in range(KC):
                        copy_xnT(cur + 1, kc)
                if has_prev:
                    for kc in range(KC):
                        act.wait_ge(xn2T_ps, prev.count(2, kc + 1 + FREE))
                        act.copy(hi[:, kc, :], ps[:, MISC, :]).then_inc(hi_sb, 1)
                    for o in range(KC):
                        act.wait_ge(ffn_ps, prev.count(2, o + 1))
                        act.activation(fT[:, o, :], ps[:, MISC, :], ACT.Identity, bias=cols[:, 3, o:o + 1],
                                       scale=cols[:, 2, o:o + 1]).then_inc(fT_sb, 1)

            for kc in range(KC):
                copy_xnT(Seq(0), kc)
            act.wait_ge(w_in, N_W)
            steps(act, step)

        @block.gpsimd
        def _(pool):
            pool.memset(neg_half[:, :], -0.5).then_inc(const_ok, 1)
            for done in (res_ok, xn2_ok, xn2T_ps, clip_sb, *stored):
                pool.sem_inc(done, FREE)
            pool.wait_ge(const_ok, 1)

            def normalize(s, src, nm, ve, rs, dst, st, rs_ok, done, used, free=0):
                pool.wait_ge(st, s.count(2, 2))
                pool.tensor_tensor(rs[:, :], ve[:, :], neg_half[:, :], ALU.pow).then_inc(rs_ok, 1)
                pool.wait_ge(rs_ok, s.count(1, 1))
                if not (s.is_(0)):
                    pool.wait_ge(used, s.count(2, free))
                pool.tensor_tensor(pool_gate[:, :], neg_half[:, 0:1], neg_half[:, 0:1], ALU.add)
                for j in range(NT):
                    ins = pool.tensor_scalar(dst[:, j, :], src[:, j, :], nm[:, j:j + 1], rs[:, j:j + 1],
                                             ALU.add, ALU.mult)
                ins.then_inc(done, 1)

            def norm1(s):
                normalize(s, xs[s.parity], nm1, ve1, rs1, xn, ln1_st, rs1_ok, xn_ok, xnT_ps)

            def step(cur, has_cur, last=False):
                has_prev = not (cur.is_(0))
                prev = cur + -1
                if has_prev:
                    pool.wait_ge(res_ok, prev.count(1, FREE))
                    pool.wait_ge(gn_st, prev.count(GN_STEPS, 9))
                    pool.tensor_tensor(grs[:, :], gve[:, :], neg_half[:, 0:KC], ALU.pow).then_inc(grs_ok, 1)
                if has_cur:
                    pool.tensor_copy(x1[cur.parity][:, :, :], xs[cur.parity][:, :, :]).then_inc(x_copied, 1)
                if not last:
                    norm1(cur + 1)
                if has_prev:
                    normalize(prev, x1[prev.parity], nm2, ve2, rs2, xn2, ln2_st, rs2_ok, xn2_ok, xn2T_ps, FREE)
                    pool.wait_ge(clip_sb, prev.count(2, 2 + FREE))
                    if not prev.is_(0):
                        pool.wait_ge(stored[prev.parity], prev.same_parity_count(16, FREE))
                    pool.tensor_tensor(res[prev.parity][:, :, :], clipped[:, :, :], x1[prev.parity][:, :, :],
                                       ALU.add).then_inc(res_ok, 1)

            norm1(Seq(0))
            steps(pool, step)


def constants():
    start, stop = np.log(1.0 / 32.0), np.log(1.0 / 512.0)
    ramp = np.linspace(start, stop, H).astype(np.float32)
    gamma = (np.float32(1.0) - np.exp(ramp)).astype(np.float64)
    power = np.arange(L) - L // 2
    by_head = gamma[:, None] ** power[None, :]
    decay_q = np.repeat(by_head, DH, axis=0).astype(np.float32)
    decay_k = np.repeat(1.0 / by_head, DH, axis=0).astype(np.float32)
    n = np.arange(P)
    same = (n[:, None] // DH) == (n[None, :] // DH)
    squares = np.stack([np.eye(P), n[:, None] <= n[None, :], same, same / DH]).astype(np.float32)
    return decay_q, decay_k, squares


def by_partition(vectors):
    return np.stack(vectors).reshape(len(vectors), KC, P).transpose(2, 0, 1)


def kernel(**inputs):
    import numpy as _np
    import concourse.bacc as _bacc
    from concourse import mybir as _mybir
    from concourse.bass_utils import run_bass_kernel_spmd as _run

    nc = _bacc.Bacc("TRN2", target_bir_lowering=False, num_devices=1)
    a = {k: _np.asarray(v) for k, v in inputs.items()}
    decay_q, decay_k, squares = constants()
    given = {
        "x": a["L0_attn_x"],
        "wq_t": a["L0_attn_Wq"].T, "wk_t": a["L0_attn_Wk"].T, "wv_t": a["L0_attn_Wv"].T,
        "wo_t": a["L0_attn_Wo"].T, "ffn_t": a["L0_ffn_weights"].T,
        "columns": by_partition([a["L0_attn_gn_weight"], a["L0_attn_gn_bias"], a["L0_ffn_scale"], a["L0_ffn_bias"]]),
        "decay_q": decay_q, "decay_k": decay_k, "squares": squares,
    }
    given = {k: _np.ascontiguousarray(v) for k, v in given.items()}
    aps = [nc.dram_tensor(k, v.shape, _mybir.dt.from_np(v.dtype), kind="ExternalInput").ap() for k, v in given.items()]
    res = nc.dram_tensor("res_out", given["x"].shape, _mybir.dt.from_np(given["x"].dtype), kind="ExternalOutput").ap()
    build(nc, *aps, res)
    r = _run(nc, [given], core_ids=[0])
    return r.results[0]["res_out"]
```

```python
from contextlib import ExitStack

import numpy as np

import concourse.bass as bass
from concourse import mybir

F32 = mybir.dt.float32
F16 = mybir.dt.float16
ALU = mybir.AluOpType
ACT = mybir.ActivationFunctionType

P = 128
B = 8
L = 512
D = 256
H = 8
DH = D // H
KC = D // P
HG = P // DH
NT = L // P
EPS = 1e-5
MAX_VAL = 100.0


class Seq:

    def __init__(self, offset, turn=None):
        self.offset, self.turn = offset, turn
        self.parity = offset % 2

    def __add__(self, k):
        return Seq(self.offset + k, self.turn)

    def count(self, each, more=0):
        fixed = self.offset * each + more
        return fixed if self.turn is None else self.turn * (2 * each) + fixed

    def same_parity_count(self, each, more=0):
        fixed = self.offset // 2 * each + more
        return fixed if self.turn is None else self.turn * each + fixed

    def is_(self, n):
        return self.turn is None and self.offset == n


def build(nc, x, wq_n, wk_n, wv_n, wo_t, ffn_t, columns, decay_q, decay_k, squares, out):
    x_v = x.rearrange("b (j p) c -> b p j c", p=P)
    out_v = out.rearrange("b (j p) c -> b p j c", p=P)
    halves = lambda w: w.rearrange("(k p) n -> p k n", p=P)

    with ExitStack() as ctx:
        def sb(name, shape, dt=F32):
            return ctx.enter_context(nc.sbuf_tensor(name, shape, dt))

        def sem(name):
            return ctx.enter_context(nc.semaphore(name))

        wn = [sb(f"wn{m}", [P, KC, D]) for m in range(3)]
        rowmax = sb("rowmax", [P, 3, KC])
        rowinv = sb("rowinv", [P, 3, KC])
        unscale = sb("unscale", [P, 3, KC])
        unscale_v2 = sb("unscale_v2", [P, KC])
        wscaled = [sb(f"wscaled{m}", [P, KC, D]) for m in range(3)]
        w16 = [sb(f"w16_{m}", [P, 2, KC, D], F16) for m in range(3)]
        w16T = [sb(f"w16T_{m}", [P, 2, KC, D], F16) for m in range(3)]
        ident16 = sb("ident16", [P, P], F16)
        wo = sb("wo", [P, KC, D])
        woscaled = sb("woscaled", [P, KC, D])
        wo16 = sb("wo16", [P, 2, KC, D], F16)
        reach = sb("reach", [P, 4])
        reach_all = sb("reach_all", [P, 2])
        reach_inv = sb("reach_inv", [P, 2])
        gn_abs = sb("gn_abs", [P, 2, KC])
        gn_cols = sb("gn_cols", [P, 2, KC])
        out_scale = sb("out_scale", [P, 1])
        wf = sb("wf", [P, KC, D])
        wpos = sb("wpos", [P, KC, D])
        wsign = sb("wsign", [P, KC, D], F16)
        cols = sb("cols", [P, 4, KC])
        dq = sb("dq", [P, KC, L])
        dk = sb("dk", [P, KC, L])
        sq = sb("sq", [P, 4, P])
        ident, causal, same_head, head_avg = (sq[:, n, :] for n in range(4))
        neg_half = sb("neg_half", [P, NT])
        dve_gate, pool_gate = sb("dve_gate", [P, 1]), sb("pool_gate", [P, 1])

        xs = [sb(f"xs{p}", [P, NT, D]) for p in range(2)]
        st1 = sb("st1", [P, NT, 6])
        mv1 = sb("mv1", [P, NT, 2])
        nm1 = sb("nm1", [P, NT])
        ve1 = sb("ve1", [P, NT])
        rs1 = sb("rs1", [P, NT])
        xn = sb("xn", [P, NT, D])
        xh = sb("xh", [P, KC, L], F16)
        xl = sb("xl", [P, KC, L], F16)
        qT = sb("qT", [P, KC, L])
        kT = sb("kT", [P, KC, L])
        ktok = sb("ktok", [P, NT, D])
        v = sb("v", [P, NT, D])
        probs = [sb(f"probs{p}", [P, HG, P]) for p in range(2)]
        state = [sb(f"state{p}", [P, KC, P]) for p in range(2)]
        gst = sb("gst", [P, KC, 6])
        gmv = sb("gmv", [P, KC, 2])
        gm = sb("gm", [P, KC])
        gv = sb("gv", [P, KC])
        gmean = sb("gmean", [P, KC])
        ga = sb("ga", [P, KC])
        gdev = sb("gdev", [P, KC])
        gdev2 = sb("gdev2", [P, KC])
        gz = sb("gz", [P, KC])
        gve = sb("gve", [P, KC])
        grs = sb("grs", [P, KC])
        gscale = sb("gscale", [P, KC])
        gms = sb("gms", [P, KC])
        gbias = sb("gbias", [P, KC])
        yn = sb("yn", [P, KC, L])
        yh = sb("yh", [P, KC, L], F16)
        yl = sb("yl", [P, KC, L], F16)
        x1 = [sb(f"x1_{p}", [P, NT, D]) for p in range(2)]
        st2 = sb("st2", [P, NT, 6])
        mv2 = sb("mv2", [P, NT, 2])
        nm2 = sb("nm2", [P, NT])
        ve2 = sb("ve2", [P, NT])
        rs2 = sb("rs2", [P, NT])
        nb2 = sb("nb2", [P, NT])
        xn2 = sb("xn2", [P, NT, D])
        hi = sb("hi", [P, KC, L], F16)
        lo = sb("lo", [P, KC, L], F16)
        fT = sb("fT", [P, KC, L])
        clipped = sb("clipped", [P, NT, D])
        res = [sb(f"res{p}", [P, NT, D]) for p in range(2)]

        ps = ctx.enter_context(nc.psum_tensor("ps", [P, 8, 512], F32))
        Y, STATE, MISC = 4, 6, 7

        w_in, squares_in = sem("w_in"), sem("squares_in")
        x_in = [sem(f"x_in{p}") for p in range(2)]
        stored = [sem(f"stored{p}") for p in range(2)]
        weight_in = [sem(f"weight_in{m}") for m in range(3)]
        set_up, w16_ok, wT_ps, wT_sb = sem("set_up"), sem("w16_ok"), sem("wT_ps"), sem("wT_sb")
        reach_ok, reach_max, wo_ok = sem("reach_ok"), sem("reach_max"), sem("wo_ok")
        xnT_ps, q_ps, k_ps, v_ps = sem("xnT_ps"), sem("q_ps"), sem("k_ps"), sem("v_ps")
        gn_ps, wo_ps, ktok_ps = sem("gn_ps"), sem("wo_ps"), sem("ktok_ps")
        scores_ps = sem("scores_ps")
        state_ps = sem("state_ps")
        y_ps = sem("y_ps")
        xn2T_ps, ffn_ps, back_ps = sem("xn2T_ps"), sem("ffn_ps"), sem("back_ps")
        aggr1, ln1_st = sem("aggr1"), sem("ln1_st")
        q_sb, k_sb = sem("q_sb"), sem("k_sb")
        gn_st = sem("gn_st")
        x1_sb = sem("x1_sb")
        aggr2, ln2_st = sem("aggr2"), sem("ln2_st")
        masked = sem("masked")
        state_sb = sem("state_sb")
        xl_sb, yh_sb, yl_sb = sem("xl_sb"), sem("yh_sb"), sem("yl_sb")
        lo_sb, clip_sb = sem("lo_sb"), sem("clip_sb")
        xh_sb, v_sb, yn_sb, ktok_sb = sem("xh_sb"), sem("v_sb"), sem("yn_sb"), sem("ktok_sb")
        hi_sb, fT_sb = sem("hi_sb"), sem("fT_sb")
        const_ok, x_copied = sem("const_ok"), sem("x_copied")
        rs1_ok, xn_ok, grs_ok, rs2_ok, nb2_ok, xn2_ok, res_ok = (
            sem(n) for n in ("rs1_ok", "xn_ok", "grs_ok", "rs2_ok", "nb2_ok", "xn2_ok", "res_ok"))
        xn2b_ok = sem("xn2b_ok")

        UNITS = NT * KC
        GN_STEPS = 16
        UNIT = 1024.0
        FITS = 2.0 ** 14
        FREE = 1
        N_W = 5 * 16

        def steps(eng, step):
            step(Seq(0), True)
            with eng.Fori(0, (B - 2) // 2) as r:
                odd = Seq(1, r)
                step(odd, True)
                step(odd + 1, True)
            step(Seq(B - 1), True, last=True)
            step(Seq(B), False, last=True)

        block = ctx.enter_context(nc.Block())

        @block.sync
        def _(sp):
            def load_x(s):
                if not s.is_(1):
                    sp.wait_ge(xn_ok, (s + -1).count(1))
                    sp.wait_ge(x_copied, (s + -1).count(1))
                sp.dma_start(xs[s.parity][:, :, :], x_v[s.count(1)]).then_inc(x_in[s.parity], 16)

            sp.dma_start(xs[0][:, :, :], x_v[0]).then_inc(x_in[0], 16)
            rows = lambda w: w.rearrange("(g p) n -> p g n", p=P)
            sp.dma_start(wn[0][:, :, :], rows(wq_n)).then_inc(weight_in[0], 16)
            sp.dma_start(sq[:, :, :], squares.rearrange("n p m -> p n m")).then_inc(squares_in, 16)
            sp.dma_start(wn[1][:, :, :], rows(wk_n)).then_inc(weight_in[1], 16)
            sp.dma_start(wn[2][:, :, :], rows(wv_n)).then_inc(weight_in[2], 16)
            for sbuf, dram in ((dq, halves(decay_q)), (dk, halves(decay_k)), (cols, columns),
                               (wo, halves(wo_t)), (wf, halves(ffn_t))):
                sp.dma_start(sbuf[:, :, :], dram).then_inc(w_in, 16)
            sp.dma_start(xs[1][:, :, :], x_v[1]).then_inc(x_in[1], 16)

            def step(cur, has_cur, last=False):
                if cur.is_(0):
                    return
                if not last:
                    load_x(cur + 1)

            steps(sp, step)
            for p in range(2):
                sp.wait_ge(stored[p], 16 * (B // 2) + FREE)

        @block.tensor
        def _(pe):
            def xn_transposes(s, kc):
                if kc == 0:
                    pe.wait_ge(xn_ok, s.count(1, 1))
                else:
                    pe.wait_ge(xl_sb, s.count(2, 1))
                for j in range(NT):
                    mm = pe.transpose(ps[:, STATE, j * P:(j + 1) * P], xn[:, j, kc * P:(kc + 1) * P], ident)
                mm.then_inc(xnT_ps, 1)

            PARTS = ((0, 0), (0, 1), (1, 0))

            def project_qk(s, m, bank, done, g, kcs=range(KC)):
                for kc in kcs:
                    if m == 0 and g == 0:
                        pe.wait_ge(xl_sb, s.count(2, kc + 1))
                    for n, (pw, px) in enumerate(PARTS):
                        mm = pe.matmul(ps[:, bank + g, :], w16T[m][:, pw, kc, g * P:(g + 1) * P],
                                       (xh, xl)[px][:, kc, :], start=(kc == 0 and n == 0),
                                       stop=(kc == KC - 1 and n == len(PARTS) - 1))
                if kc == KC - 1:
                    mm.then_inc(done, 1)

            def project_v(s, half):
                bank = (MISC, STATE)[half]
                for j in range(2):
                    t, n = 2 * half + j, 0
                    for px, pw in PARTS:
                        for kc in range(KC):
                            mm = pe.matmul(ps[:, bank, j * D:(j + 1) * D], (xh, xl)[px][:, kc, t * P:(t + 1) * P],
                                           w16T[2][:, pw, kc, :], start=(n == 0), stop=(n == 3 * KC - 1))
                            n += 1
                mm.then_inc(v_ps, 1)

            def out_projection(s, half):
                for j in range(2):
                    t, n = 2 * half + j, 0
                    for py, pw in PARTS:
                        for kc in range(KC):
                            mm = pe.matmul(ps[:, Y + half, j * D:(j + 1) * D], (yh, yl)[py][:, kc, t * P:(t + 1) * P],
                                           wo16[:, pw, kc, :], start=(n == 0), stop=(n == 3 * KC - 1))
                            n += 1
                mm.then_inc(wo_ps, 1)

            def k_transposes(s, half):
                for j in range(2):
                    c = 2 * half + j
                    for g in range(KC):
                        mm = pe.transpose(ps[:, 2 + half, j * D + g * P:j * D + (g + 1) * P],
                                          kT[:, g, c * P:(c + 1) * P], ident)
                mm.then_inc(ktok_ps, 1)

            def scores(s, u):
                c, g = divmod(u, KC)
                for h in range(HG):
                    if u and h % 2 == 0:
                        pe.wait_ge(masked, s.count(2 * UNITS, 2 * u - 1 + h // 2))
                    rows = slice(h * DH, (h + 1) * DH)
                    mm = pe.matmul(ps[:, h, 0:P], kT[rows, g, c * P:(c + 1) * P], qT[rows, g, c * P:(c + 1) * P],
                                   start=True, stop=True)
                    if h % 2:
                        mm.then_inc(scores_ps, 1)

            def update_state(s, c):
                if c == 0:
                    pe.wait_ge(v_sb, s.count(2, 2))
                    pe.wait_ge(ktok_sb, s.count(2, 1))
                else:
                    pe.wait_ge(state_sb, s.count(3, c))
                for g in range(KC):
                    mm = pe.matmul(ps[:, STATE, g * P:(g + 1) * P], ktok[:, c, g * P:(g + 1) * P],
                                   v[:, c, g * P:(g + 1) * P], start=(c == 0 and g == 0), stop=(c == NT - 2),
                                   skip_group_check=True)
                mm.then_inc(state_ps, 1)

            def outputs(s, u):
                c, g = divmod(u, KC)
                ys = ps[:, Y + g, c * P:(c + 1) * P]
                if c:
                    if g == 0:
                        pe.wait_ge(state_sb, s.count(3, c))
                    pe.matmul(ys, state[(c - 1) % 2][:, g, :], qT[:, g, c * P:(c + 1) * P],
                              start=True, stop=False, skip_group_check=True)
                for h in range(HG):
                    mm = pe.matmul(ps[h * DH:(h + 1) * DH, Y + g, c * P:(c + 1) * P],
                                   v[:, c, g * P + h * DH:g * P + (h + 1) * DH], probs[u % 2][:, h, :],
                                   start=(c == 0), stop=True, skip_group_check=True)
                if c == NT - 1:
                    mm.then_inc(y_ps, 1)

            def xn2_transposes(s, kc):
                if kc == 0:
                    pe.wait_ge(xn2_ok, s.count(1, 1 + FREE))
                    pe.wait_ge(xn2b_ok, s.count(1, 1))
                for j in range(NT):
                    mm = pe.transpose(ps[:, MISC, j * P:(j + 1) * P], xn2[:, j, kc * P:(kc + 1) * P], ident)
                mm.then_inc(xn2T_ps, 1)

            def ffn(s, o):
                n = 0
                for part in (hi, lo):
                    for kc in range(KC):
                        mm = pe.matmul(ps[:, MISC, :], wsign[:, kc, o * P:(o + 1) * P], part[:, kc, :],
                                       start=(n == 0), stop=(n == 2 * KC - 1))
                        n += 1
                mm.then_inc(ffn_ps, 1)

            def back_transposes(s, half):
                for j in range(2):
                    t = 2 * half + j
                    for o in range(KC):
                        mm = pe.transpose(ps[:, MISC, j * D + o * P:j * D + (o + 1) * P],
                                          fT[:, o, t * P:(t + 1) * P], ident)
                mm.then_inc(back_ps, 1)

            def second_half(s, n):
                if n == 0:
                    xn2_transposes(s, 0)
                elif n == 1:
                    pe.wait_ge(lo_sb, s.count(2, 1))
                    xn2_transposes(s, 1)
                elif n == 2:
                    pe.wait_ge(lo_sb, s.count(2, 2))
                    ffn(s, 0)
                elif n == 3:
                    pe.wait_ge(fT_sb, s.count(2, 1))
                    ffn(s, 1)
                elif n == 4:
                    pe.wait_ge(fT_sb, s.count(2, 2))
                    back_transposes(s, 0)
                elif n == 5:
                    pe.wait_ge(clip_sb, s.count(2, 1 + FREE))
                    back_transposes(s, 1)

            def step(cur, has_cur, last=False):
                has_prev = not cur.is_(0)
                prev = cur + -1
                if has_cur:
                    project_qk(cur, 0, 0, q_ps, 1)
                if has_prev:
                    pe.wait_ge(gn_st, prev.count(GN_STEPS, 6))
                    pe.matmul(ps[:, STATE, 0:KC], head_avg, gm[:, :], start=True, stop=True).then_inc(gn_ps, 1)
                if has_cur:
                    project_qk(cur, 1, 2, k_ps, 0, (0,))
                if has_prev:
                    pe.wait_ge(gn_st, prev.count(GN_STEPS, 10))
                    pe.matmul(ps[:, STATE, 0:KC], head_avg, gz[:, :], start=True, stop=True).then_inc(gn_ps, 1)
                if has_cur:
                    project_qk(cur, 1, 2, k_ps, 0, (1,))
                    project_qk(cur, 1, 2, k_ps, 1)
                    if has_prev and not cur.is_(1):
                        pe.wait_ge(clip_sb, prev.count(2, FREE))
                    project_v(cur, 0)
                    if has_prev:
                        pe.wait_ge(gn_st, prev.count(GN_STEPS, 11))
                    project_v(cur, 1)
                    pe.wait_ge(k_sb, cur.count(2, 2))
                    for half in range(2):
                        k_transposes(cur, half)
                if has_prev:
                    if cur.is_(1):
                        pe.wait_ge(wo_ok, 1)
                    pe.wait_ge(yl_sb, prev.count(2, 2))
                    out_projection(prev, 0)
                if has_cur:
                    pe.wait_ge(q_sb, cur.count(2, 2))
                    pe.wait_ge(ktok_sb, cur.count(2, 2))
                    scores(cur, 0)
                if has_prev:
                    out_projection(prev, 1)
                if not has_cur:
                    pe.wait_ge(clip_sb, prev.count(2, FREE))
                    for n in range(6):
                        second_half(prev, n)
                    return
                update_state(cur, 0)
                for u in range(UNITS):
                    c, g = divmod(u, KC)
                    if u + 1 < UNITS:
                        scores(cur, u + 1)
                    pe.wait_ge(masked, cur.count(2 * UNITS, 2 * u + 2))
                    if has_prev and c == 0:
                        pe.wait_ge(x1_sb, prev.count(2, 1 + g))
                    outputs(cur, u)
                    if g == 0 and 0 < c < NT - 1:
                        update_state(cur, c)
                    if u >= 3 and has_prev:
                        second_half(prev, u - 3)
                    if u == 7 and not last:
                        project_qk(cur + 1, 0, 0, q_ps, 0)
                    if u == 7 and has_prev:
                        second_half(prev, 5)
                    if u in (5, 6) and not last:
                        if u == 5:
                            pe.wait_ge(state_sb, cur.count(3, 3))
                        xn_transposes(cur + 1, u - 5)

            pe.wait_ge(squares_in, 16)
            for m in range(3):
                pe.wait_ge(w16_ok, m + 1)
                bank = ps[:, m, :].bitcast(F16).rearrange("p (h k d) -> p h k d", h=2, k=KC)
                for part in range(2):
                    for kc in range(KC):
                        for g in range(KC):
                            mm = pe.transpose(bank[:, part, kc, g * P:(g + 1) * P],
                                              w16[m][:, part, g, kc * P:(kc + 1) * P], ident16[:, :])
                mm.then_inc(wT_ps, 1)
                if m == 0:
                    for kc in range(KC):
                        xn_transposes(Seq(0), kc)
            pe.wait_ge(wT_sb, 3)
            project_qk(Seq(0), 0, 0, q_ps, 0)
            steps(pe, step)

        @block.vector
        def _(dve):
            def ln_tile(j, src, st, aggr):
                dve.bn_stats(st[:, j, :], src[:, j, :]).then_inc(aggr, 1)

            def ln_sums(s, st, mv, nm, ve, aggr, done):
                dve.wait_ge(aggr, s.count(2 * NT, NT))
                dve.memset(dve_gate[:, :], 0.0)
                for j in range(NT):
                    dve.bn_aggr(mv[:, j, :], st[:, j, :]).then_inc(aggr, 1)
                dve.wait_ge(aggr, s.count(2 * NT, 2 * NT))
                dve.tensor_scalar(ve[:, :], mv[:, :, 1], EPS, None, ALU.add).then_inc(done, 1)
                dve.tensor_scalar(nm[:, :], mv[:, :, 0], -1.0, None, ALU.mult).then_inc(done, 1)

            def ln1_tiles(s, tiles):
                if 0 in tiles:
                    dve.wait_ge(x_in[s.parity], s.same_parity_count(16, 16))
                    if not s.is_(0):
                        dve.wait_ge(xn_ok, s.count(1))
                for j in tiles:
                    ln_tile(j, xs[s.parity], st1, aggr1)

            def ln1_sums(s):
                ln_sums(s, st1, mv1, nm1, ve1, aggr1, ln1_st)

            def ln2_tile(s, j):
                dve.wait_ge(x1_sb, s.count(2, 1 + j // 2))
                if j == 0 and not s.is_(0):
                    dve.wait_ge(xn2_ok, s.count(1, FREE))
                    dve.wait_ge(xn2T_ps, s.count(2, FREE))
                ln_tile(j, x1[s.parity], st2, aggr2)

            def ln2_sums(s):
                ln_sums(s, st2, mv2, nm2, ve2, aggr2, ln2_st)

            def decayed(s, g, bank, seen, table, dst, done):
                dve.wait_ge(seen, s.count(2, g + 1))
                dve.tensor_tensor(dst[:, g, :], ps[:, bank + g, :], table[:, g, :], ALU.mult).then_inc(done, 1)

            def gn_row(s, g):
                dve.wait_ge(y_ps, s.count(2, g + 1))
                dve.bn_stats(gst[:, g, :], ps[:, Y + g, :]).then_inc(gn_st, 1)

            def gn_rows(s):
                dve.wait_ge(gn_st, s.count(GN_STEPS, 2))
                dve.memset(dve_gate[:, :], 0.0)
                for g in range(KC):
                    dve.bn_aggr(gmv[:, g, :], gst[:, g, :]).then_inc(gn_st, 1)
                dve.wait_ge(gn_st, s.count(GN_STEPS, 4))
                dve.tensor_tensor(gm[:, :], gmv[:, :, 0], unscale[:, 2, :], ALU.mult).then_inc(gn_st, 1)
                dve.tensor_tensor(gv[:, :], gmv[:, :, 1], unscale_v2[:, :], ALU.mult).then_inc(gn_st, 1)

            def gn_deviation(s):
                dve.wait_ge(gn_ps, s.count(2, 1))
                dve.tensor_tensor(gdev[:, :], ps[:, STATE, 0:KC], gm[:, :], ALU.subtract).then_inc(gn_st, 1)
                dve.tensor_copy(gmean[:, :], ps[:, STATE, 0:KC]).then_inc(gn_st, 1)
                dve.wait_ge(gn_st, s.count(GN_STEPS, 8))
                dve.tensor_tensor(gdev2[:, :], gdev[:, :], gdev[:, :], ALU.mult).then_inc(gn_st, 1)
                dve.wait_ge(gn_st, s.count(GN_STEPS, 9))
                dve.tensor_tensor(gz[:, :], gdev2[:, :], gv[:, :], ALU.add).then_inc(gn_st, 1)

            def gn_variance(s):
                dve.wait_ge(gn_ps, s.count(2, 2))
                dve.tensor_scalar(gve[:, :], ps[:, STATE, 0:KC], EPS, None, ALU.add).then_inc(gn_st, 1)

            def gn_affine(s):
                dve.wait_ge(grs_ok, s.count(1, 1))
                dve.tensor_tensor(ga[:, :], grs[:, :], gn_cols[:, 0, :], ALU.mult).then_inc(gn_st, 1)
                dve.wait_ge(gn_st, s.count(GN_STEPS, 12))
                dve.tensor_tensor(gscale[:, :], ga[:, :], unscale[:, 2, :], ALU.mult).then_inc(gn_st, 1)
                dve.tensor_tensor(gms[:, :], gmean[:, :], ga[:, :], ALU.mult).then_inc(gn_st, 1)
                dve.wait_ge(gn_st, s.count(GN_STEPS, 14))
                dve.tensor_tensor(gbias[:, :], gn_cols[:, 1, :], gms[:, :], ALU.subtract).then_inc(gn_st, 2)

            def split_yn(s, g):
                dve.wait_ge(yn_sb, s.count(2, g + 1))
                dve.tensor_copy(yh[:, g, :], yn[:, g, :]).then_inc(yh_sb, 1)
                dve.wait_ge(yh_sb, s.count(2, g + 1))
                dve.tensor_tensor(yl[:, g, :], yn[:, g, :], yh[:, g, :], ALU.subtract).then_inc(yl_sb, 1)

            def residual(s, half):
                dve.wait_ge(wo_ps, s.count(2, half + 1))
                if half == 0:
                    dve.wait_ge(x_copied, s.count(1, 1))
                j = slice(2 * half, 2 * half + 2)
                dve.scalar_tensor_tensor(x1[s.parity][:, j, :], ps[:, Y + half, :].rearrange("p (j c) -> p j c", j=2),
                                         out_scale[:, :], x1[s.parity][:, j, :], ALU.mult, ALU.add).then_inc(x1_sb, 1)

            def mask(s, u):
                for pair in range(2):
                    dve.wait_ge(scores_ps, s.count(2 * UNITS, 2 * u + pair + 1))
                    dve.tensor_tensor(probs[u % 2][:, 2 * pair:2 * pair + 2, :], ps[:, 2 * pair:2 * pair + 2, 0:P],
                                      causal.rearrange("p (a t) -> p a t", a=1).broadcast_to([P, 2, P]),
                                      ALU.mult).then_inc(masked, 1)

            def copy_state(s, c):
                dve.wait_ge(state_ps, s.count(3, c + 1))
                dve.tensor_tensor(state[c % 2][:, :, :], ps[:, STATE, 0:KC * P].rearrange("p (g n) -> p g n", g=KC),
                                  same_head.rearrange("p (a t) -> p a t", a=1).broadcast_to([P, KC, P]),
                                  ALU.mult).then_inc(state_sb, 1)

            def xn_low(s, kc):
                dve.wait_ge(xh_sb, s.count(2, kc + 1))
                dve.tensor_tensor(xl[:, kc, :], ps[:, STATE, :], xh[:, kc, :], ALU.subtract).then_inc(xl_sb, 1)

            def low_part(s, kc):
                dve.wait_ge(hi_sb, s.count(2, kc + 1))
                dve.tensor_tensor(lo[:, kc, :], ps[:, MISC, :], hi[:, kc, :], ALU.subtract).then_inc(lo_sb, 1)

            def clip(s, half):
                dve.wait_ge(back_ps, s.count(2, half + 1))
                if half == 0 and not (s.is_(0)):
                    dve.wait_ge(res_ok, s.count(1, FREE))
                dve.tensor_scalar(clipped[:, 2 * half:2 * half + 2, :],
                                  ps[:, MISC, :].rearrange("p (j c) -> p j c", j=2),
                                  MAX_VAL, -MAX_VAL, ALU.min, ALU.max).then_inc(clip_sb, 1)

            def step(cur, has_cur, last=False):
                has_prev = not (cur.is_(0))
                prev = cur + -1
                if has_prev:
                    gn_deviation(prev)
                if has_cur:
                    decayed(cur, 0, 0, q_ps, dq, qT, q_sb)
                if has_prev:
                    gn_variance(prev)
                if has_cur:
                    decayed(cur, 1, 0, q_ps, dq, qT, q_sb)
                if has_prev:
                    gn_affine(prev)
                if has_cur:
                    decayed(cur, 0, 2, k_ps, dk, kT, k_sb)
                    decayed(cur, 1, 2, k_ps, dk, kT, k_sb)
                if has_prev:
                    split_yn(prev, 0)
                    split_yn(prev, 1)
                if not last:
                    ln1_tiles(cur + 1, range(NT))
                    ln1_sums(cur + 1)
                if has_prev:
                    residual(prev, 0)
                    ln2_tile(prev, 0)
                if not has_cur:
                    ln2_tile(prev, 1)
                    residual(prev, 1)
                    ln2_tile(prev, 2)
                    ln2_tile(prev, 3)
                    ln2_sums(prev)
                    low_part(prev, 0)
                    low_part(prev, 1)
                    clip(prev, 0)
                    clip(prev, 1)
                    return
                for u in range(UNITS):
                    mask(cur, u)
                    if u in (1, 3, 5):
                        copy_state(cur, u // 2)
                    if has_prev:
                        if u == 0:
                            residual(prev, 1)
                            ln2_tile(prev, 1)
                        if u in (1, 2):
                            ln2_tile(prev, u + 1)
                        if u == 2:
                            ln2_sums(prev)
                        if u in (4, 5):
                            low_part(prev, u - 4)
                    if u in (6, 7) and not last:
                        xn_low(cur + 1, u - 6)
                    if u == 7 and has_prev:
                        clip(prev, 0)
                    if u == 7:
                        gn_row(cur, 0)
                        gn_row(cur, 1)
                        gn_rows(cur)
                        if has_prev:
                            clip(prev, 1)

            ln1_tiles(Seq(0), range(NT))
            ln1_sums(Seq(0))

            chain = [0]

            def after(ins):
                chain[0] += 1
                ins.then_inc(set_up, 1)
                dve.wait_ge(set_up, chain[0])

            dve.wait_ge(squares_in, 16)
            after(dve.tensor_copy(ident16[:, :], ident))
            for m in range(3):
                dve.wait_ge(weight_in[m], 16)
                after(dve.tensor_reduce(rowmax[:, m, :], wn[m][:, :, :], mybir.AxisListType.X, ALU.max,
                                        apply_absolute_value=True))
                after(dve.tensor_scalar(unscale[:, m, :], rowmax[:, m, :], 1e-30, 1.0 / UNIT, ALU.max, ALU.mult))
                after(dve.reciprocal(rowinv[:, m, :], unscale[:, m, :]))
                for g in range(KC):
                    ins = dve.tensor_scalar(wscaled[m][:, g, :], wn[m][:, g, :], rowinv[:, m, g:g + 1], None,
                                            ALU.mult)
                after(ins)
                after(dve.tensor_copy(w16[m][:, 0, :, :], wscaled[m][:, :, :]))
                dve.tensor_tensor(w16[m][:, 1, :, :], wscaled[m][:, :, :], w16[m][:, 0, :, :],
                                  ALU.subtract).then_inc(w16_ok, 1)
                if m == 0:
                    xn_low(Seq(0), 0)
                    xn_low(Seq(0), 1)
            dve.wait_ge(w_in, N_W)
            after(dve.tensor_tensor(unscale_v2[:, :], unscale[:, 2, :], unscale[:, 2, :], ALU.mult))
            for table, m in ((dq, 0), (dk, 1)):
                for g in range(KC):
                    ins = dve.tensor_scalar(table[:, g, :], table[:, g, :], unscale[:, m, g:g + 1], None, ALU.mult)
            after(ins)
            after(dve.tensor_reduce(reach[:, 0:1], wo[:, :, :], mybir.AxisListType.XY, ALU.max,
                                    apply_absolute_value=True))
            after(dve.tensor_scalar(gn_abs[:, :, :], cols[:, 0:2, :], -1.0, None, ALU.mult))
            after(dve.tensor_tensor(gn_abs[:, :, :], gn_abs[:, :, :], cols[:, 0:2, :], ALU.max))
            after(dve.scalar_tensor_tensor(reach[:, 2:4], gn_abs[:, 0, :], float(L * DH) ** 0.5, gn_abs[:, 1, :],
                                           ALU.mult, ALU.add))
            dve.tensor_reduce(reach[:, 1:2], reach[:, 2:4], mybir.AxisListType.X, ALU.max).then_inc(reach_ok, 1)
            dve.wait_ge(reach_max, 1)
            after(dve.tensor_scalar(reach_all[:, :], reach_all[:, :], 1e-30, None, ALU.max))
            after(dve.reciprocal(reach_inv[:, :], reach_all[:, :]))
            after(dve.tensor_scalar(out_scale[:, :], reach_all[:, 0:1], reach_all[:, 1:2], 1.0 / (UNIT * FITS),
                                    ALU.mult, ALU.mult))
            after(dve.tensor_scalar(woscaled[:, :, :], wo[:, :, :], reach_inv[:, 0:1], UNIT, ALU.mult, ALU.mult))
            after(dve.tensor_scalar(gn_cols[:, :, :], cols[:, 0:2, :], reach_inv[:, 1:2], FITS, ALU.mult, ALU.mult))
            after(dve.tensor_copy(wo16[:, 0, :, :], woscaled[:, :, :]))
            after(dve.tensor_tensor(wo16[:, 1, :, :], woscaled[:, :, :], wo16[:, 0, :, :], ALU.subtract))
            after(dve.tensor_scalar(wpos[:, :, :], wf[:, :, :], 0.0, 2.0, ALU.is_ge, ALU.mult))
            dve.tensor_scalar(wsign[:, :, :], wpos[:, :, :], -1.0, None, ALU.add).then_inc(wo_ok, 1)
            steps(dve, step)

        @block.scalar
        def _(act):
            def copy_xh(s, kc):
                act.wait_ge(xnT_ps, s.count(2, kc + 1))
                act.copy(xh[:, kc, :], ps[:, STATE, :]).then_inc(xh_sb, 1)

            def step(cur, has_cur, last=False):
                has_prev = not (cur.is_(0))
                prev = cur + -1
                if has_prev:
                    act.wait_ge(gn_st, prev.count(GN_STEPS, GN_STEPS))
                    for g in range(KC):
                        act.activation(yn[:, g, :], ps[:, Y + g, :], ACT.Identity, bias=gbias[:, g:g + 1],
                                       scale=gscale[:, g:g + 1]).then_inc(yn_sb, 1)
                if has_cur:
                    act.wait_ge(x_in[cur.parity], cur.same_parity_count(16, 16))
                    act.copy(x1[cur.parity][:, :, :], xs[cur.parity][:, :, :]).then_inc(x_copied, 1)
                if has_cur:
                    for half in range(2):
                        act.wait_ge(v_ps, cur.count(2, half + 1))
                        act.copy(v[:, 2 * half:2 * half + 2, :],
                                 ps[:, (MISC, STATE)[half], :].rearrange("p (j c) -> p j c", j=2)).then_inc(v_sb, 1)
                    for half in range(2):
                        act.wait_ge(ktok_ps, cur.count(2, half + 1))
                        act.copy(ktok[:, 2 * half:2 * half + 2, :],
                                 ps[:, 2 + half, :].rearrange("p (j c) -> p j c", j=2)).then_inc(ktok_sb, 1)
                if has_prev:
                    act.wait_ge(nb2_ok, prev.count(1, 1))
                    if not prev.is_(0):
                        act.wait_ge(xn2T_ps, prev.count(2, FREE))
                    for j in range(NT // 2, NT):
                        ins = act.activation(xn2[:, j, :], x1[prev.parity][:, j, :], ACT.Identity,
                                             bias=nb2[:, j:j + 1], scale=rs2[:, j:j + 1])
                    ins.then_inc(xn2b_ok, 1)
                    for kc in range(KC):
                        act.wait_ge(xn2T_ps, prev.count(2, kc + 1 + FREE))
                        act.copy(hi[:, kc, :], ps[:, MISC, :]).then_inc(hi_sb, 1)
                for o in range(KC):
                    if has_prev:
                        act.wait_ge(ffn_ps, prev.count(2, o + 1))
                        act.activation(fT[:, o, :], ps[:, MISC, :], ACT.Identity, bias=cols[:, 3, o:o + 1],
                                       scale=cols[:, 2, o:o + 1]).then_inc(fT_sb, 1)
                    if not last:
                        copy_xh(cur + 1, o)
                if has_prev:
                    act.wait_ge(res_ok, prev.count(1, 1 + FREE))
                    act.dma_start(out_v[prev.count(1)], res[prev.parity][:, :, :]).then_inc(stored[prev.parity], 16)

            for m in range(3):
                act.wait_ge(wT_ps, m + 1)
                act.copy(w16T[m][:, :, :, :].rearrange("p h k d -> p (h k d)"),
                         ps[:, m, :].bitcast(F16)).then_inc(wT_sb, 1)
                if m == 0:
                    for kc in range(KC):
                        copy_xh(Seq(0), kc)
            act.wait_ge(w_in, N_W)
            steps(act, step)

        @block.gpsimd
        def _(pool):
            pool.memset(neg_half[:, :], -0.5).then_inc(const_ok, 1)
            for done in (res_ok, xn2_ok, xn2T_ps, clip_sb, *stored):
                pool.sem_inc(done, FREE)
            pool.wait_ge(const_ok, 1)

            def norm1(s):
                pool.wait_ge(ln1_st, s.count(2, 2))
                pool.tensor_tensor(rs1[:, :], ve1[:, :], neg_half[:, :], ALU.pow).then_inc(rs1_ok, 1)
                pool.wait_ge(rs1_ok, s.count(1, 1))
                if not s.is_(0):
                    pool.wait_ge(xnT_ps, s.count(2))
                pool.tensor_tensor(pool_gate[:, :], neg_half[:, 0:1], neg_half[:, 0:1], ALU.add)
                for j in range(NT):
                    ins = pool.tensor_scalar(xn[:, j, :], xs[s.parity][:, j, :], nm1[:, j:j + 1], rs1[:, j:j + 1],
                                             ALU.add, ALU.mult)
                ins.then_inc(xn_ok, 1)

            def norm2(s):
                pool.wait_ge(ln2_st, s.count(2, 2))
                pool.tensor_tensor(rs2[:, :], ve2[:, :], neg_half[:, :], ALU.pow).then_inc(rs2_ok, 1)
                pool.wait_ge(rs2_ok, s.count(1, 1))
                if not s.is_(0):
                    pool.wait_ge(xn2T_ps, s.count(2, FREE))
                pool.tensor_tensor(nb2[:, :], nm2[:, :], rs2[:, :], ALU.mult).then_inc(nb2_ok, 1)
                for j in range(NT // 2):
                    ins = pool.tensor_scalar(xn2[:, j, :], x1[s.parity][:, j, :], nm2[:, j:j + 1], rs2[:, j:j + 1],
                                             ALU.add, ALU.mult)
                ins.then_inc(xn2_ok, 1)

            def step(cur, has_cur, last=False):
                has_prev = not (cur.is_(0))
                prev = cur + -1
                if has_prev:
                    pool.wait_ge(gn_st, prev.count(GN_STEPS, 11))
                    pool.tensor_tensor(grs[:, :], gve[:, :], neg_half[:, 0:KC], ALU.pow).then_inc(grs_ok, 1)
                if not last:
                    norm1(cur + 1)
                if has_prev:
                    norm2(prev)
                    pool.wait_ge(clip_sb, prev.count(2, 2 + FREE))
                    if not prev.is_(0):
                        pool.wait_ge(stored[prev.parity], prev.same_parity_count(16, FREE))
                    pool.tensor_tensor(res[prev.parity][:, :, :], clipped[:, :, :], x1[prev.parity][:, :, :],
                                       ALU.add).then_inc(res_ok, 1)

            norm1(Seq(0))
            pool.wait_ge(reach_ok, 1)
            pool.partition_all_reduce(reach_all[:, :], reach[:, 0:2], P, bass.bass_isa.ReduceOp.max).then_inc(reach_max, 1)
            steps(pool, step)


def constants():
    start, stop = np.log(1.0 / 32.0), np.log(1.0 / 512.0)
    ramp = np.linspace(start, stop, H).astype(np.float32)
    gamma = (np.float32(1.0) - np.exp(ramp)).astype(np.float64)
    power = np.arange(L) - L // 2
    by_head = gamma[:, None] ** power[None, :]
    decay_q = np.repeat(by_head, DH, axis=0).astype(np.float32)
    decay_k = np.repeat(1.0 / by_head, DH, axis=0).astype(np.float32)
    n = np.arange(P)
    same = (n[:, None] // DH) == (n[None, :] // DH)
    squares = np.stack([np.eye(P), n[:, None] <= n[None, :], same, same / DH]).astype(np.float32)
    return decay_q, decay_k, squares


def by_partition(vectors):
    return np.stack(vectors).reshape(len(vectors), KC, P).transpose(2, 0, 1)


def kernel(**inputs):
    import numpy as _np
    import concourse.bacc as _bacc
    from concourse import mybir as _mybir
    from concourse.bass_utils import run_bass_kernel_spmd as _run

    nc = _bacc.Bacc("TRN2", target_bir_lowering=False, num_devices=1)
    a = {k: _np.asarray(v) for k, v in inputs.items()}
    decay_q, decay_k, squares = constants()
    given = {
        "x": a["L0_attn_x"],
        "wq": a["L0_attn_Wq"], "wk": a["L0_attn_Wk"], "wv": a["L0_attn_Wv"],
        "wo_t": a["L0_attn_Wo"].T, "ffn_t": a["L0_ffn_weights"].T,
        "columns": by_partition([a["L0_attn_gn_weight"], a["L0_attn_gn_bias"], a["L0_ffn_scale"], a["L0_ffn_bias"]]),
        "decay_q": decay_q, "decay_k": decay_k, "squares": squares,
    }
    given = {k: _np.ascontiguousarray(v) for k, v in given.items()}
    aps = [nc.dram_tensor(k, v.shape, _mybir.dt.from_np(v.dtype), kind="ExternalInput").ap() for k, v in given.items()]
    res = nc.dram_tensor("res_out", given["x"].shape, _mybir.dt.from_np(given["x"].dtype), kind="ExternalOutput").ap()
    build(nc, *aps, res)
    r = _run(nc, [given], core_ids=[0])
    return r.results[0]["res_out"]
```

```python
from contextlib import ExitStack

import numpy as np

import concourse.bass as bass
from concourse import mybir

F32 = mybir.dt.float32
F16 = mybir.dt.float16
ALU = mybir.AluOpType
ACT = mybir.ActivationFunctionType

P = 128
B = 8
L = 512
D = 256
H = 8
DH = D // H
KC = D // P
HG = P // DH
NT = L // P
EPS = 1e-5
MAX_VAL = 100.0




class Seq:

    def __init__(self, offset, turn=None):
        self.offset, self.turn = offset, turn
        self.parity = offset % 2

    def __add__(self, k):
        return Seq(self.offset + k, self.turn)

    def count(self, each, more=0):
        fixed = self.offset * each + more
        return fixed if self.turn is None else self.turn * (2 * each) + fixed

    def same_parity_count(self, each, more=0):
        fixed = self.offset // 2 * each + more
        return fixed if self.turn is None else self.turn * each + fixed

    def is_(self, n):
        return self.turn is None and self.offset == n


def build(nc, x, wq_n, wk_n, wv_n, wo_t, ffn_t, columns, ffn_rows, decay_q, decay_k, squares, out):
    x_v = x.rearrange("b (j p) c -> b p j c", p=P)
    out_v = out.rearrange("b (j p) c -> b p j c", p=P)
    halves = lambda w: w.rearrange("(k p) n -> p k n", p=P)

    with ExitStack() as ctx:
        def sb(name, shape, dt=F32):
            return ctx.enter_context(nc.sbuf_tensor(name, shape, dt))

        def sem(name):
            return ctx.enter_context(nc.semaphore(name))

        wn = [sb(f"wn{m}", [P, KC, D]) for m in range(3)]
        rowmax = sb("rowmax", [P, 3, KC])
        rowinv = sb("rowinv", [P, 3, KC])
        unscale = sb("unscale", [P, 3, KC])
        unscale_v = sb("unscale_v", [P, KC])
        unscale_v2 = sb("unscale_v2", [P, KC])
        w16 = [sb(f"w16_{m}", [P, 2, KC, D], F16) for m in range(3)]
        w16T = [sb(f"w16T_{m}", [P, 2, KC, D], F16) for m in range(3)]
        ident16 = sb("ident16", [P, P], F16)
        wo = sb("wo", [P, KC, D])
        wo16 = sb("wo16", [P, 2, KC, D], F16)
        reach = sb("reach", [P, 4])
        reach_all = sb("reach_all", [P, 2])
        reach_inv = sb("reach_inv", [P, 2])
        wo_factor = sb("wo_factor", [P, 1])
        gn_abs = sb("gn_abs", [P, 2, KC])
        gn_cols = sb("gn_cols", [P, 2, KC])
        out_scale = sb("out_scale", [P, 1])
        wf = sb("wf", [P, KC, D])
        wpos = sb("wpos", [P, KC, D])
        wsign = sb("wsign", [P, KC, D], F16)
        cols = sb("cols", [P, 2, KC])
        rows_f = sb("rows_f", [P, 2, D])
        dq = sb("dq", [P, KC, L])
        dk = sb("dk", [P, KC, L])
        sq = sb("sq", [P, 4, P])
        ident, causal, same_head, head_avg = (sq[:, n, :] for n in range(4))
        neg_half = sb("neg_half", [P, NT])
        dve_gate, pool_gate = sb("dve_gate", [P, 1]), sb("pool_gate", [P, 1])

        xs = [sb(f"xs{p}", [P, NT, D]) for p in range(2)]
        st1 = sb("st1", [P, NT, 6])
        mv1 = sb("mv1", [P, NT, 2])
        nm1 = sb("nm1", [P, NT])
        ve1 = sb("ve1", [P, NT])
        rs1 = sb("rs1", [P, NT])
        xn = sb("xn", [P, NT, D])
        xh = sb("xh", [P, KC, L], F16)
        xl = sb("xl", [P, KC, L], F16)
        qT = sb("qT", [P, KC, L])
        kT = sb("kT", [P, KC, L])
        ktok = sb("ktok", [P, NT, D])
        v = sb("v", [P, NT, D])
        probs = [sb(f"probs{p}", [P, HG, P]) for p in range(2)]
        state = [sb(f"state{p}", [P, KC, P]) for p in range(2)]
        gst = sb("gst", [P, KC, 6])
        gmv = sb("gmv", [P, KC, 2])
        gm = sb("gm", [P, KC])
        gv = sb("gv", [P, KC])
        gmean = sb("gmean", [P, KC])
        ga = sb("ga", [P, KC])
        gdev = sb("gdev", [P, KC])
        gdev2 = sb("gdev2", [P, KC])
        gz = sb("gz", [P, KC])
        gve = sb("gve", [P, KC])
        grs = sb("grs", [P, KC])
        gscale = sb("gscale", [P, KC])
        gms = sb("gms", [P, KC])
        gbias = sb("gbias", [P, KC])
        yn = sb("yn", [P, KC, L])
        yh = sb("yh", [P, KC, L], F16)
        yl = sb("yl", [P, KC, L], F16)
        x1 = [sb(f"x1_{p}", [P, NT, D]) for p in range(2)]
        st2 = sb("st2", [P, NT, 6])
        mv2 = sb("mv2", [P, NT, 2])
        nm2 = sb("nm2", [P, NT])
        ve2 = sb("ve2", [P, NT])
        rs2 = sb("rs2", [P, NT])
        nb2 = sb("nb2", [P, NT])
        xn2 = sb("xn2", [P, NT, D])
        hi = sb("hi", [P, KC, L], F16)
        lo = sb("lo", [P, KC, L], F16)
        f = sb("f", [P, NT, D])
        res = [sb(f"res{p}", [P, NT, D]) for p in range(2)]

        ps = ctx.enter_context(nc.psum_tensor("ps", [P, 8, 512], F32))
        Y, STATE, MISC = 4, 6, 7

        w_in, squares_in, tables_in = sem("w_in"), sem("squares_in"), sem("tables_in")
        x_in = [sem(f"x_in{p}") for p in range(2)]
        first_x_in = sem("first_x_in")
        stored = [sem(f"stored{p}") for p in range(2)]
        weight_in = [sem(f"weight_in{m}") for m in range(3)]
        rowmax_ok, unscale_ok, rowinv_ok = sem("rowmax_ok"), sem("unscale_ok"), sem("rowinv_ok")
        w16_hi, w16_ok, wT_ps, wT_sb = sem("w16_hi"), sem("w16_ok"), sem("wT_ps"), sem("wT_sb")
        set_up, ident16_ok, tables_ok = sem("set_up"), sem("ident16_ok"), sem("tables_ok")
        wo_factor_ok, wo_hi = sem("wo_factor_ok"), sem("wo_hi")
        reach_ok, reach_max = sem("reach_ok"), sem("reach_max")
        xnT_ps, q_ps, k_ps, v_ps = sem("xnT_ps"), sem("q_ps"), sem("k_ps"), sem("v_ps")
        ktok_ps, wo_ps, xn2T_ps, ffn_ps = sem("ktok_ps"), sem("wo_ps"), sem("xn2T_ps"), sem("ffn_ps")
        y_ps, gn_ps = sem("y_ps"), sem("gn_ps")
        scores_ps = sem("scores_ps")
        state_ps = sem("state_ps")
        ln1_st, ln2_st = sem("ln1_st"), sem("ln2_st")
        q_sb, k_sb, xl_sb, yl_sb = sem("q_sb"), sem("k_sb"), sem("xl_sb"), sem("yl_sb")
        x1_sb, lo_sb, ffn_sb, clip_sb = sem("x1_sb"), sem("lo_sb"), sem("ffn_sb"), sem("clip_sb")
        aggr1, aggr2 = sem("aggr1"), sem("aggr2")
        gn_st = sem("gn_st")
        masked = sem("masked")
        state_sb = sem("state_sb")
        first_xn = sem("first_xn")
        last_yn, last_yh, last_aggr2 = sem("last_yn"), sem("last_yh"), sem("last_aggr2")
        xh_sb, v_sb, ktok_sb = sem("xh_sb"), sem("v_sb"), sem("ktok_sb")
        yn_sb, yh_sb, hi_sb = sem("yn_sb"), sem("yh_sb"), sem("hi_sb")
        x_copied, xn2b_ok = sem("x_copied"), sem("xn2b_ok")
        const_ok = sem("const_ok")
        rs1_ok, xn_ok, grs_ok = sem("rs1_ok"), sem("xn_ok"), sem("grs_ok")
        rs2_ok, nb2_ok, xn2_ok = sem("rs2_ok"), sem("nb2_ok"), sem("xn2_ok")
        bias_ok = sem("bias_ok")
        res_ok = sem("res_ok")

        UNITS = NT * KC
        GN_MEANS, GN_SQUARES, GN_VARIANCE, GN_STEPS = 6, 10, 11, 16
        UNIT = 1024.0
        NORM = 2.0 ** 11
        FITS = 2.0 ** 14
        FREE = 1
        N_W = 4 * 16

        def steps(eng, step):
            step(Seq(0), True)
            with eng.Fori(0, (B - 2) // 2) as r:
                odd = Seq(1, r)
                step(odd, True)
                step(odd + 1, True)
            step(Seq(B - 1), True, last=True)
            step(Seq(B), False, last=True)

        block = ctx.enter_context(nc.Block())

        LAST = Seq(B - 1)
        tokens = lambda half: slice(half * L // 2, (half + 1) * L // 2)
        LAST_WO, LAST_XN2T, LAST_FFN = (0, 1, 2, 3), (STATE, MISC, STATE, MISC), (Y, Y + 1, Y, Y + 1)

        def by_tile(n):
            return rows_f[:, n, :].rearrange("p (a d) -> p a d", a=1).broadcast_to([P, 2, D])

        def xn_bank(s, kc):
            return MISC if s.is_(0) and kc == 1 else STATE

        def add_x1(eng, s, half):
            eng.wait_ge(clip_sb, s.count(2, half + 1))
            if not s.is_(0):
                eng.wait_ge(stored[s.parity], s.same_parity_count(16, FREE))
            j = slice(2 * half, 2 * half + 2)
            eng.tensor_tensor(res[s.parity][:, j, :], f[:, j, :], x1[s.parity][:, j, :], ALU.add).then_inc(res_ok, 1)

        @block.sync
        def _(sp):
            def load_x(s):
                sp.wait_ge(xn_ok, (s + -1).count(1))
                sp.wait_ge(x_copied, (s + -1).count(1))
                sp.dma_start(xs[s.parity][:, :, :], x_v[s.count(1)]).then_inc(x_in[s.parity], 16)

            sp.dma_start(xs[0][:, 0:2, :], x_v[0][:, 0:2, :]).then_inc(first_x_in, 16)
            sp.dma_start(xs[0][:, 2:4, :], x_v[0][:, 2:4, :]).then_inc(x_in[0], 16)
            rows = lambda w: w.rearrange("(g p) n -> p g n", p=P)
            sp.dma_start(wn[0][:, :, :], rows(wq_n)).then_inc(weight_in[0], 16)
            sp.dma_start(wn[1][:, :, :], rows(wk_n)).then_inc(weight_in[1], 16)
            sp.dma_start(sq[:, :, :], squares.rearrange("n p m -> p n m")).then_inc(squares_in, 16)
            sp.dma_start(wn[2][:, :, :], rows(wv_n)).then_inc(weight_in[2], 16)
            sp.dma_start(dq[:, :, :], halves(decay_q)).then_inc(tables_in, 16)
            sp.dma_start(dk[:, :, :], halves(decay_k)).then_inc(tables_in, 16)
            for sbuf, dram in ((cols, columns), (wo, halves(wo_t)), (wf, halves(ffn_t)), (rows_f, ffn_rows)):
                sp.dma_start(sbuf[:, :, :], dram).then_inc(w_in, 16)
            sp.dma_start(xs[1][:, :, :], x_v[1]).then_inc(x_in[1], 16)

            def step(cur, has_cur, last=False):
                if not (cur.is_(0) or last):
                    load_x(cur + 1)

            steps(sp, step)
            for t in range(NT):
                sp.wait_ge(res_ok, LAST.count(2, t + 1 + FREE))
                sp.dma_start(out_v[B - 1][:, t, :], res[LAST.parity][:, t, :]).then_inc(stored[LAST.parity], 16)
            for p in range(2):
                sp.wait_ge(stored[p], 16 * (B // 2 + (NT - 1) * (p == LAST.parity)) + FREE)

        @block.tensor
        def _(pe):
            def first_xn_transposes():
                for j in range(NT):
                    pe.wait_ge(first_xn, j + 1)
                    for kc in range(KC):
                        mm = pe.transpose(ps[:, xn_bank(Seq(0), kc), j * P:(j + 1) * P],
                                          xn[:, j, kc * P:(kc + 1) * P], ident)
                        if j == NT - 1:
                            mm.then_inc(xnT_ps, 1)

            def xn_transposes(s, kc):
                if kc == 0:
                    pe.wait_ge(xn_ok, s.count(1, 1))
                else:
                    pe.wait_ge(xl_sb, s.count(2, 1))
                for j in range(NT):
                    mm = pe.transpose(ps[:, STATE, j * P:(j + 1) * P], xn[:, j, kc * P:(kc + 1) * P], ident)
                mm.then_inc(xnT_ps, 1)

            PARTS = ((0, 0), (0, 1), (1, 0))

            def project_qk(s, m, bank, done, g, kcs=range(KC)):
                for kc in kcs:
                    if m == 0 and g == 0:
                        pe.wait_ge(xl_sb, s.count(2, kc + 1))
                    for n, (pw, px) in enumerate(PARTS):
                        mm = pe.matmul(ps[:, bank + g, :], w16T[m][:, pw, kc, g * P:(g + 1) * P],
                                       (xh, xl)[px][:, kc, :], start=(kc == 0 and n == 0),
                                       stop=(kc == KC - 1 and n == len(PARTS) - 1))
                if kc == KC - 1:
                    mm.then_inc(done, 1)

            def project_v(s, half):
                bank = (MISC, STATE)[half]
                for j in range(2):
                    t, n = 2 * half + j, 0
                    for px, pw in PARTS:
                        for kc in range(KC):
                            mm = pe.matmul(ps[:, bank, j * D:(j + 1) * D], (xh, xl)[px][:, kc, t * P:(t + 1) * P],
                                           w16T[2][:, pw, kc, :], start=(n == 0), stop=(n == 3 * KC - 1))
                            n += 1
                mm.then_inc(v_ps, 1)

            def out_projection_tile(t, dst):
                n = 0
                for py, pw in PARTS:
                    for kc in range(KC):
                        mm = pe.matmul(dst, (yh, yl)[py][:, kc, t * P:(t + 1) * P], wo16[:, pw, kc, :],
                                       start=(n == 0), stop=(n == 3 * KC - 1))
                        n += 1
                return mm

            def out_projection(s, half):
                for j in range(2):
                    mm = out_projection_tile(2 * half + j, ps[:, Y + half, j * D:(j + 1) * D])
                mm.then_inc(wo_ps, 1)

            def k_transposes(s, half):
                for j in range(2):
                    c = 2 * half + j
                    for g in range(KC):
                        mm = pe.transpose(ps[:, 2 + half, j * D + g * P:j * D + (g + 1) * P],
                                          kT[:, g, c * P:(c + 1) * P], ident)
                mm.then_inc(ktok_ps, 1)

            def scores(s, u):
                c, g = divmod(u, KC)
                for h in range(HG):
                    if u and h % 2 == 0:
                        pe.wait_ge(masked, s.count(2 * UNITS, 2 * u - 1 + h // 2))
                    rows = slice(h * DH, (h + 1) * DH)
                    mm = pe.matmul(ps[:, h, 0:P], kT[rows, g, c * P:(c + 1) * P], qT[rows, g, c * P:(c + 1) * P],
                                   start=True, stop=True)
                    if h % 2:
                        mm.then_inc(scores_ps, 1)

            def update_state(s, c):
                if c == 0:
                    pe.wait_ge(v_sb, s.count(2, 2))
                    pe.wait_ge(ktok_sb, s.count(2, 1))
                else:
                    pe.wait_ge(state_sb, s.count(3, c))
                for g in range(KC):
                    mm = pe.matmul(ps[:, STATE, g * P:(g + 1) * P], ktok[:, c, g * P:(g + 1) * P],
                                   v[:, c, g * P:(g + 1) * P], start=(c == 0 and g == 0), stop=(c == NT - 2),
                                   skip_group_check=True)
                mm.then_inc(state_ps, 1)

            def outputs(s, u):
                c, g = divmod(u, KC)
                ys = ps[:, Y + g, c * P:(c + 1) * P]
                if c:
                    if g == 0:
                        pe.wait_ge(state_sb, s.count(3, c))
                    pe.matmul(ys, state[(c - 1) % 2][:, g, :], qT[:, g, c * P:(c + 1) * P],
                              start=True, stop=False, skip_group_check=True)
                for h in range(HG):
                    mm = pe.matmul(ps[h * DH:(h + 1) * DH, Y + g, c * P:(c + 1) * P],
                                   v[:, c, g * P + h * DH:g * P + (h + 1) * DH], probs[u % 2][:, h, :],
                                   start=(c == 0), stop=True, skip_group_check=True)
                if c == NT - 1:
                    mm.then_inc(y_ps, 1)

            def xn2_transposes(s, kc):
                if kc == 0:
                    pe.wait_ge(xn2_ok, s.count(1, 1 + FREE))
                    pe.wait_ge(xn2b_ok, s.count(1, 1))
                for j in range(NT):
                    mm = pe.transpose(ps[:, MISC, j * P:(j + 1) * P], xn2[:, j, kc * P:(kc + 1) * P], ident)
                mm.then_inc(xn2T_ps, 1)

            def ffn_tile(t, dst):
                n = 0
                for part in (hi, lo):
                    for kc in range(KC):
                        mm = pe.matmul(dst, part[:, kc, t * P:(t + 1) * P], wsign[:, kc, :],
                                       start=(n == 0), stop=(n == 2 * KC - 1))
                        n += 1
                return mm

            def ffn(s, half):
                for j in range(2):
                    mm = ffn_tile(2 * half + j, ps[:, MISC, j * D:(j + 1) * D])
                mm.then_inc(ffn_ps, 1)

            def second_half(s, n):
                if n == 0:
                    xn2_transposes(s, 0)
                elif n == 1:
                    pe.wait_ge(lo_sb, s.count(2, 1))
                    xn2_transposes(s, 1)
                elif n == 2:
                    pe.wait_ge(lo_sb, s.count(2, 2))
                    ffn(s, 0)
                elif n == 3:
                    pe.wait_ge(ffn_sb, s.count(2, 1 + FREE))
                    ffn(s, 1)

            def head_averages(s, n):
                pe.wait_ge(gn_st, s.count(GN_STEPS, (GN_MEANS, GN_SQUARES)[n]))
                pe.matmul(ps[:, STATE, 0:KC], head_avg, (gm, gz)[n][:, :], start=True, stop=True).then_inc(gn_ps, 1)

            def last_xn2_transposes(t):
                pe.wait_ge(xn2_ok, LAST.count(1, t + 1 + FREE))
                if t == 0:
                    pe.wait_ge(gn_st, LAST.count(GN_STEPS, GN_VARIANCE))
                elif t == 1:
                    pe.wait_ge(ffn_sb, LAST.count(2, FREE))
                else:
                    pe.wait_ge(lo_sb, LAST.count(2, t - 1))
                for kc in range(KC):
                    mm = pe.transpose(ps[:, LAST_XN2T[t], kc * P:(kc + 1) * P], xn2[:, t, kc * P:(kc + 1) * P], ident)
                mm.then_inc(xn2T_ps, 1)

            def last_ffn(t):
                pe.wait_ge(lo_sb, LAST.count(2, t + 1))
                if t >= 2:
                    pe.wait_ge(ffn_sb, LAST.count(2, t - 1 + FREE))
                ffn_tile(t, ps[:, LAST_FFN[t], 0:D]).then_inc(ffn_ps, 1)

            def finish_last():
                for t in range(NT):
                    if t % 2 == 0:
                        pe.wait_ge(yl_sb, LAST.count(2, t // 2 + 1))
                    out_projection_tile(t, ps[:, LAST_WO[t], 0:D]).then_inc(wo_ps, 1)
                last_xn2_transposes(0)
                last_xn2_transposes(1)
                for t in range(NT):
                    last_ffn(t)
                    if t + 2 < NT:
                        last_xn2_transposes(t + 2)

            def step(cur, has_cur, last=False):
                if not has_cur:
                    return finish_last()
                has_prev = not cur.is_(0)
                prev = cur + -1
                if cur.is_(0):
                    pe.wait_ge(wT_sb, 2)
                project_qk(cur, 1, 2, k_ps, 0, (0, 1) if cur.is_(0) else (1,))
                project_qk(cur, 1, 2, k_ps, 1)
                if cur.is_(0):
                    pe.wait_ge(wT_sb, 3)
                else:
                    pe.wait_ge(ffn_sb, prev.count(2, FREE))
                project_v(cur, 0)
                if has_prev:
                    pe.wait_ge(gn_st, prev.count(GN_STEPS, GN_VARIANCE))
                    project_v(cur, 1)
                pe.wait_ge(k_sb, cur.count(2, 2))
                for half in range(2):
                    k_transposes(cur, half)
                if not has_prev:
                    project_v(cur, 1)
                if has_prev:
                    pe.wait_ge(yl_sb, prev.count(2, 2))
                    out_projection(prev, 0)
                pe.wait_ge(q_sb, cur.count(2, 2))
                pe.wait_ge(ktok_sb, cur.count(2, 2))
                scores(cur, 0)
                if has_prev:
                    out_projection(prev, 1)
                for u in range(UNITS):
                    c, g = divmod(u, KC)
                    if u + 1 < UNITS:
                        scores(cur, u + 1)
                    if u >= 4 and has_prev and not (u == 7 and last):
                        second_half(prev, u - 4)
                    pe.wait_ge(masked, cur.count(2 * UNITS, 2 * u + 2))
                    if has_prev and c == 0:
                        pe.wait_ge(x1_sb, prev.count(2, 1 + g))
                    outputs(cur, u)
                    if g == 0 and c < NT - 1:
                        update_state(cur, c)
                    if u in (5, 6) and not last:
                        if u == 5:
                            pe.wait_ge(state_sb, cur.count(3, 3))
                        xn_transposes(cur + 1, u - 5)
                if last:
                    second_half(prev, 3)
                    head_averages(cur, 0)
                    head_averages(cur, 1)
                    return
                project_qk(cur + 1, 0, 0, q_ps, 0)
                project_qk(cur + 1, 0, 0, q_ps, 1, (0,))
                head_averages(cur, 0)
                project_qk(cur + 1, 0, 0, q_ps, 1, (1,))
                project_qk(cur + 1, 1, 2, k_ps, 0, (0,))
                head_averages(cur, 1)

            def weight_transposes(m):
                if m == 2:
                    pe.wait_ge(wT_sb, 1)
                pe.wait_ge(w16_ok, m + 1)
                bank = ps[:, Y + m % 2, :].bitcast(F16).rearrange("p (h k d) -> p h k d", h=2, k=KC)
                for part in range(2):
                    for kc in range(KC):
                        for g in range(KC):
                            mm = pe.transpose(bank[:, part, kc, g * P:(g + 1) * P],
                                              w16[m][:, part, g, kc * P:(kc + 1) * P], ident16[:, :])
                mm.then_inc(wT_ps, 1)

            pe.wait_ge(squares_in, 16)
            first_xn_transposes()
            pe.wait_ge(ident16_ok, 1)
            weight_transposes(0)
            weight_transposes(1)
            pe.wait_ge(wT_sb, 1)
            project_qk(Seq(0), 0, 0, q_ps, 0)
            weight_transposes(2)
            project_qk(Seq(0), 0, 0, q_ps, 1)
            steps(pe, step)

        @block.vector
        def _(dve):
            def ln_tile(j, src, st, aggr):
                dve.bn_stats(st[:, j, :], src[:, j, :]).then_inc(aggr, 1)

            def ln_sums(s, st, mv, nm, ve, aggr, done):
                dve.wait_ge(aggr, s.count(2 * NT, NT))
                dve.memset(dve_gate[:, :], 0.0)
                for j in range(NT):
                    dve.bn_aggr(mv[:, j, :], st[:, j, :]).then_inc(aggr, 1)
                dve.wait_ge(aggr, s.count(2 * NT, 2 * NT))
                dve.tensor_scalar(ve[:, :], mv[:, :, 1], EPS, NORM ** -2, ALU.add, ALU.mult).then_inc(done, 1)
                dve.tensor_scalar(nm[:, :], mv[:, :, 0], -1.0, None, ALU.mult).then_inc(done, 1)

            def ln1_tiles(s, tiles):
                if 0 in tiles:
                    dve.wait_ge(x_in[s.parity], s.same_parity_count(16, 16))
                    if not s.is_(0):
                        dve.wait_ge(xn_ok, s.count(1))
                for j in tiles:
                    ln_tile(j, xs[s.parity], st1, aggr1)

            def ln1_sums(s):
                ln_sums(s, st1, mv1, nm1, ve1, aggr1, ln1_st)

            def ln2_tile(s, j):
                dve.wait_ge(x1_sb, s.count(2, 1 + j // 2))
                if j == 0 and not s.is_(0):
                    dve.wait_ge(xn2_ok, s.count(1, FREE))
                    dve.wait_ge(xn2T_ps, s.count(2, FREE))
                ln_tile(j, x1[s.parity], st2, aggr2)

            def ln2_sums(s):
                ln_sums(s, st2, mv2, nm2, ve2, aggr2, ln2_st)

            def decayed(s, g, bank, seen, table, dst, done):
                dve.wait_ge(seen, s.count(2, g + 1))
                dve.tensor_tensor(dst[:, g, :], ps[:, bank + g, :], table[:, g, :], ALU.mult).then_inc(done, 1)

            def gn_row(s, g):
                dve.wait_ge(y_ps, s.count(2, g + 1))
                dve.bn_stats(gst[:, g, :], ps[:, Y + g, :]).then_inc(gn_st, 1)

            def gn_rows(s):
                dve.wait_ge(gn_st, s.count(GN_STEPS, 2))
                dve.memset(dve_gate[:, :], 0.0)
                for g in range(KC):
                    dve.bn_aggr(gmv[:, g, :], gst[:, g, :]).then_inc(gn_st, 1)
                dve.wait_ge(gn_st, s.count(GN_STEPS, 4))
                dve.tensor_tensor(gm[:, :], gmv[:, :, 0], unscale_v[:, :], ALU.mult).then_inc(gn_st, 1)
                dve.tensor_tensor(gv[:, :], gmv[:, :, 1], unscale_v2[:, :], ALU.mult).then_inc(gn_st, 1)

            def gn_deviation(s):
                dve.wait_ge(gn_ps, s.count(2, 1))
                dve.tensor_tensor(gdev[:, :], ps[:, STATE, 0:KC], gm[:, :], ALU.subtract).then_inc(gn_st, 1)
                dve.tensor_copy(gmean[:, :], ps[:, STATE, 0:KC]).then_inc(gn_st, 1)
                dve.wait_ge(gn_st, s.count(GN_STEPS, 8))
                dve.tensor_tensor(gdev2[:, :], gdev[:, :], gdev[:, :], ALU.mult).then_inc(gn_st, 1)
                dve.wait_ge(gn_st, s.count(GN_STEPS, 9))
                dve.tensor_tensor(gz[:, :], gdev2[:, :], gv[:, :], ALU.add).then_inc(gn_st, 1)

            def gn_variance(s):
                dve.wait_ge(gn_ps, s.count(2, 2))
                dve.tensor_scalar(gve[:, :], ps[:, STATE, 0:KC], EPS, None, ALU.add).then_inc(gn_st, 1)

            def gn_affine(s):
                dve.wait_ge(grs_ok, s.count(1, 1))
                dve.tensor_tensor(ga[:, :], grs[:, :], gn_cols[:, 0, :], ALU.mult).then_inc(gn_st, 1)
                dve.wait_ge(gn_st, s.count(GN_STEPS, 12))
                dve.tensor_tensor(gscale[:, :], ga[:, :], unscale_v[:, :], ALU.mult).then_inc(gn_st, 1)
                dve.tensor_tensor(gms[:, :], gmean[:, :], ga[:, :], ALU.mult).then_inc(gn_st, 1)
                dve.wait_ge(gn_st, s.count(GN_STEPS, 14))
                dve.tensor_tensor(gbias[:, :], gn_cols[:, 1, :], gms[:, :], ALU.subtract).then_inc(gn_st, 2)

            def split_yn(s, g):
                dve.wait_ge(yh_sb, s.count(2, g + 1))
                dve.tensor_tensor(yl[:, g, :], yn[:, g, :], yh[:, g, :], ALU.subtract).then_inc(yl_sb, 1)

            def residual(s, half):
                dve.wait_ge(wo_ps, s.count(2, half + 1))
                if half == 0:
                    dve.wait_ge(x_copied, s.count(1, 1))
                j = slice(2 * half, 2 * half + 2)
                dve.scalar_tensor_tensor(x1[s.parity][:, j, :], ps[:, Y + half, :].rearrange("p (j c) -> p j c", j=2),
                                         out_scale[:, :], x1[s.parity][:, j, :], ALU.mult, ALU.add).then_inc(x1_sb, 1)

            def mask(s, u):
                for pair in range(2):
                    dve.wait_ge(scores_ps, s.count(2 * UNITS, 2 * u + pair + 1))
                    dve.tensor_tensor(probs[u % 2][:, 2 * pair:2 * pair + 2, :], ps[:, 2 * pair:2 * pair + 2, 0:P],
                                      causal.rearrange("p (a t) -> p a t", a=1).broadcast_to([P, 2, P]),
                                      ALU.mult).then_inc(masked, 1)

            def copy_state(s, c):
                dve.wait_ge(state_ps, s.count(3, c + 1))
                dve.tensor_tensor(state[c % 2][:, :, :], ps[:, STATE, 0:KC * P].rearrange("p (g n) -> p g n", g=KC),
                                  same_head.rearrange("p (a t) -> p a t", a=1).broadcast_to([P, KC, P]),
                                  ALU.mult).then_inc(state_sb, 1)

            def xn_low(s, kc):
                dve.wait_ge(xh_sb, s.count(2, kc + 1))
                dve.tensor_tensor(xl[:, kc, :], ps[:, xn_bank(s, kc), :], xh[:, kc, :], ALU.subtract).then_inc(xl_sb, 1)

            def low_part(s, kc):
                dve.wait_ge(hi_sb, s.count(2, kc + 1))
                dve.tensor_tensor(lo[:, kc, :], ps[:, MISC, :], hi[:, kc, :], ALU.subtract).then_inc(lo_sb, 1)

            def scale_ffn(s, half):
                dve.wait_ge(ffn_ps, s.count(2, half + 1))
                if half == 0 and not s.is_(0):
                    dve.wait_ge(res_ok, s.count(2, FREE))
                dve.tensor_tensor(f[:, 2 * half:2 * half + 2, :], ps[:, MISC, :].rearrange("p (j c) -> p j c", j=2),
                                  by_tile(0), ALU.mult).then_inc(ffn_sb, 1)

            def clip(s, half):
                dve.wait_ge(bias_ok, s.count(2, half + 1))
                j = slice(2 * half, 2 * half + 2)
                dve.tensor_scalar(f[:, j, :], f[:, j, :], MAX_VAL, -MAX_VAL, ALU.min, ALU.max).then_inc(clip_sb, 1)

            def last_y(half):
                dve.tensor_scalar(yn[:, 1, tokens(half)], ps[:, Y + 1, tokens(half)], gscale[:, 1:2], gbias[:, 1:2],
                                  ALU.mult, ALU.add).then_inc(last_yn, 1)
                dve.wait_ge(last_yn, half + 1)
                dve.tensor_copy(yh[:, 1, tokens(half)], yn[:, 1, tokens(half)]).then_inc(last_yh, 1)
                dve.wait_ge(last_yh, half + 1)
                dve.wait_ge(yh_sb, LAST.count(2, half + 1))
                dve.tensor_tensor(yl[:, :, tokens(half)], yn[:, :, tokens(half)], yh[:, :, tokens(half)],
                                  ALU.subtract).then_inc(yl_sb, 1)

            def last_residual(t):
                dve.wait_ge(wo_ps, LAST.count(2, t + 1))
                if t == 0:
                    dve.wait_ge(x_copied, LAST.count(1, 1))
                dve.scalar_tensor_tensor(x1[LAST.parity][:, t, :], ps[:, LAST_WO[t], 0:D], out_scale[:, :],
                                         x1[LAST.parity][:, t, :], ALU.mult, ALU.add).then_inc(x1_sb, 1)

            def last_bn(t):
                if t == 0:
                    dve.wait_ge(xn2_ok, LAST.count(1, FREE))
                    dve.wait_ge(xn2T_ps, LAST.count(2, FREE))
                dve.wait_ge(x1_sb, LAST.count(2, t + 1))
                ln_tile(t, x1[LAST.parity], st2, aggr2)

            def last_aggr(t):
                dve.wait_ge(aggr2, LAST.count(2 * NT, t + 1))
                dve.bn_aggr(mv2[:, t, :], st2[:, t, :]).then_inc(last_aggr2, 1)

            def last_sums(t):
                dve.wait_ge(last_aggr2, t + 1)
                dve.tensor_scalar(ve2[:, t:t + 1], mv2[:, t, 1:2], EPS, NORM ** -2, ALU.add, ALU.mult).then_inc(ln2_st, 1)
                dve.tensor_scalar(nm2[:, t:t + 1], mv2[:, t, 0:1], -1.0, None, ALU.mult).then_inc(ln2_st, 1)

            def last_norm2(t):
                dve.wait_ge(rs2_ok, LAST.count(1, t + 1))
                dve.wait_ge(ln2_st, LAST.count(2, 2 * t + 2))
                dve.tensor_scalar(xn2[:, t, :], x1[LAST.parity][:, t, :], nm2[:, t:t + 1], rs2[:, t:t + 1],
                                  ALU.add, ALU.mult).then_inc(xn2_ok, 1)

            def last_low(t):
                dve.wait_ge(hi_sb, LAST.count(2, t + 1))
                dve.tensor_tensor(lo[:, :, t * P:(t + 1) * P],
                                  ps[:, LAST_XN2T[t], 0:D].rearrange("p (k t) -> p k t", k=KC),
                                  hi[:, :, t * P:(t + 1) * P], ALU.subtract).then_inc(lo_sb, 1)

            def last_scale(t):
                dve.wait_ge(ffn_ps, LAST.count(2, t + 1))
                dve.tensor_tensor(f[:, t, :], ps[:, LAST_FFN[t], 0:D], rows_f[:, 0, :], ALU.mult).then_inc(ffn_sb, 1)

            def last_bias(t):
                dve.wait_ge(ffn_sb, LAST.count(2, t + 1 + FREE))
                dve.tensor_tensor(f[:, t, :], f[:, t, :], rows_f[:, 1, :], ALU.add).then_inc(bias_ok, 1)

            def last_clip(t):
                dve.wait_ge(bias_ok, LAST.count(2, t + 1))
                dve.tensor_scalar(f[:, t, :], f[:, t, :], MAX_VAL, -MAX_VAL, ALU.min, ALU.max).then_inc(clip_sb, 1)

            def last_add_x1(t):
                dve.wait_ge(clip_sb, LAST.count(2, t + 1))
                dve.tensor_tensor(res[LAST.parity][:, t, :], f[:, t, :], x1[LAST.parity][:, t, :],
                                  ALU.add).then_inc(res_ok, 1)

            def finish_last():
                gn_affine(LAST)
                dve.wait_ge(gn_st, LAST.count(GN_STEPS, GN_STEPS))
                last_y(0)
                last_y(1)
                clip(LAST + -1, 0)
                clip(LAST + -1, 1)
                last_residual(0)
                add_x1(dve, LAST + -1, 1)
                last_bn(0)
                last_residual(1)
                last_aggr(0)
                last_bn(1)
                last_sums(0)
                last_aggr(1)
                last_residual(2)
                last_sums(1)
                last_bn(2)
                last_norm2(0)
                last_aggr(2)
                last_residual(3)
                last_sums(2)
                last_bn(3)
                last_norm2(1)
                last_aggr(3)
                last_low(0)
                last_sums(3)
                last_norm2(2)
                last_low(1)
                last_norm2(3)
                dve.wait_ge(res_ok, LAST.count(2, FREE))
                dve.wait_ge(stored[LAST.parity], LAST.same_parity_count(16, FREE))
                last_scale(0)
                last_low(2)
                last_bias(0)
                last_scale(1)
                last_clip(0)
                last_bias(1)
                last_add_x1(0)
                last_low(3)
                last_clip(1)
                last_scale(2)
                last_add_x1(1)
                last_bias(2)
                last_scale(3)
                last_clip(2)
                last_bias(3)
                last_add_x1(2)
                last_clip(3)
                last_add_x1(3)

            chain = [0]

            def after(ins):
                chain[0] += 1
                ins.then_inc(set_up, 1)
                dve.wait_ge(set_up, chain[0])

            def output_weights(part):
                if part == 0:
                    dve.wait_ge(w_in, N_W)
                    dve.tensor_scalar(unscale_v[:, :], unscale[:, 2, :], 1.0 / NORM, None, ALU.mult)
                    dve.tensor_reduce(reach[:, 0:1], wo[:, :, :], mybir.AxisListType.XY, ALU.max,
                                      apply_absolute_value=True)
                    after(dve.tensor_scalar(gn_abs[:, :, :], cols[:, 0:2, :], -1.0, None, ALU.mult))
                    dve.tensor_tensor(unscale_v2[:, :], unscale_v[:, :], unscale_v[:, :], ALU.mult)
                    after(dve.tensor_tensor(gn_abs[:, :, :], gn_abs[:, :, :], cols[:, 0:2, :], ALU.max))
                    after(dve.scalar_tensor_tensor(reach[:, 2:4], gn_abs[:, 0, :], float(L * DH) ** 0.5,
                                                   gn_abs[:, 1, :], ALU.mult, ALU.add))
                    dve.tensor_reduce(reach[:, 1:2], reach[:, 2:4], mybir.AxisListType.X, ALU.max).then_inc(reach_ok, 1)
                elif part == 1:
                    dve.wait_ge(reach_max, 1)
                    after(dve.tensor_scalar(reach_all[:, :], reach_all[:, :], 1e-30, None, ALU.max))
                    after(dve.reciprocal(reach_inv[:, :], reach_all[:, :]))
                    dve.tensor_scalar(wo_factor[:, :], reach_inv[:, 0:1], UNIT, None, ALU.mult).then_inc(wo_factor_ok, 1)
                    dve.tensor_scalar(out_scale[:, :], reach_all[:, 0:1], reach_all[:, 1:2], 1.0 / (UNIT * FITS),
                                      ALU.mult, ALU.mult)
                    after(dve.tensor_scalar(gn_cols[:, :, :], cols[:, 0:2, :], reach_inv[:, 1:2], FITS, ALU.mult,
                                            ALU.mult))
                elif part == 2:
                    dve.wait_ge(wo_factor_ok, 1)
                    dve.wait_ge(wo_hi, 1)
                    dve.scalar_tensor_tensor(wo16[:, 1, :, :], wo[:, :, :], wo_factor[:, :], wo16[:, 0, :, :],
                                             ALU.mult, ALU.subtract)
                    dve.tensor_scalar(rows_f[:, 0, :], rows_f[:, 0, :], 1.0 / NORM, None, ALU.mult)
                    after(dve.tensor_scalar(wpos[:, :, :], wf[:, :, :], 0.0, 2.0, ALU.is_ge, ALU.mult))
                    dve.tensor_scalar(wsign[:, :, :], wpos[:, :, :], -1.0, None, ALU.add)

            def step(cur, has_cur, last=False):
                has_prev = not cur.is_(0)
                prev = cur + -1
                if not has_cur:
                    return finish_last()
                decayed(cur, 0, 0, q_ps, dq, qT, q_sb)
                if has_prev:
                    gn_affine(prev)
                else:
                    decayed(cur, 1, 0, q_ps, dq, qT, q_sb)
                for g in range(KC):
                    decayed(cur, g, 2, k_ps, dk, kT, k_sb)
                if has_prev:
                    decayed(cur, 1, 0, q_ps, dq, qT, q_sb)
                    split_yn(prev, 0)
                    split_yn(prev, 1)
                if not last:
                    ln1_tiles(cur + 1, range(NT))
                    ln1_sums(cur + 1)
                if cur.is_(0):
                    output_weights(0)
                if has_prev:
                    residual(prev, 0)
                    ln2_tile(prev, 0)
                for u in range(UNITS):
                    mask(cur, u)
                    if cur.is_(0) and u in (2, 4):
                        output_weights(u // 2)
                    if u in (1, 3):
                        copy_state(cur, u // 2)
                    if has_prev:
                        if u == 0:
                            residual(prev, 1)
                            ln2_tile(prev, 1)
                        if u in (1, 2):
                            ln2_tile(prev, u + 1)
                        if u == 2:
                            ln2_sums(prev)
                        if u in (5, 6):
                            low_part(prev, u - 5)
                    if u == 5:
                        copy_state(cur, 2)
                    if u == 6 and not last:
                        xn_low(cur + 1, 0)
                if last:
                    scale_ffn(prev, 0)
                    gn_row(cur, 0)
                    gn_row(cur, 1)
                    gn_rows(cur)
                    gn_deviation(cur)
                    scale_ffn(prev, 1)
                    gn_variance(cur)
                    return
                if has_prev:
                    scale_ffn(prev, 0)
                gn_row(cur, 0)
                xn_low(cur + 1, 1)
                if has_prev:
                    scale_ffn(prev, 1)
                gn_row(cur, 1)
                gn_rows(cur)
                if has_prev:
                    clip(prev, 0)
                    clip(prev, 1)
                gn_deviation(cur)
                if has_prev:
                    add_x1(dve, prev, 1)
                gn_variance(cur)

            def row_maxima(m):
                dve.wait_ge(weight_in[m], 16)
                dve.tensor_reduce(rowmax[:, m, :], wn[m][:, :, :], mybir.AxisListType.X, ALU.max,
                                  apply_absolute_value=True).then_inc(rowmax_ok, 1)

            def row_unscale(a, b):
                dve.wait_ge(rowmax_ok, b)
                dve.tensor_scalar(unscale[:, a:b, :], rowmax[:, a:b, :], 1e-30, 1.0 / UNIT, ALU.max,
                                  ALU.mult).then_inc(unscale_ok, b - a)

            def row_inverse(a, b):
                dve.wait_ge(unscale_ok, b)
                dve.reciprocal(rowinv[:, a:b, :], unscale[:, a:b, :]).then_inc(rowinv_ok, b - a)

            def weight_low(m):
                dve.wait_ge(rowinv_ok, m + 1)
                dve.wait_ge(w16_hi, m + 1)
                for g in range(KC):
                    ins = dve.scalar_tensor_tensor(w16[m][:, 1, g, :], wn[m][:, g, :], rowinv[:, m, g:g + 1],
                                                   w16[m][:, 0, g, :], ALU.mult, ALU.subtract)
                ins.then_inc(w16_ok, 1)

            def first_norm(j):
                dve.tensor_scalar(xn[:, j, :], xs[0][:, j, :], nm1[:, j:j + 1], rs1[:, j:j + 1],
                                  ALU.add, ALU.mult).then_inc(first_xn, 1)

            dve.wait_ge(first_x_in, 16)
            for j in range(NT):
                if j == 2:
                    dve.wait_ge(x_in[0], 16)
                ln_tile(j, xs[0], st1, aggr1)
            row_maxima(0)
            ln1_sums(Seq(0))
            row_maxima(1)
            row_unscale(0, 2)
            row_inverse(0, 2)
            dve.wait_ge(rs1_ok, 1)
            dve.wait_ge(ln1_st, 2)
            for j in range(NT):
                first_norm(j)
            dve.wait_ge(squares_in, 16)
            dve.tensor_copy(ident16[:, :], ident).then_inc(ident16_ok, 1)
            weight_low(0)
            dve.wait_ge(first_xn, NT)
            dve.sem_inc(xn_ok, 1)
            row_maxima(2)
            row_unscale(2, 3)
            weight_low(1)
            row_inverse(2, 3)
            xn_low(Seq(0), 0)
            xn_low(Seq(0), 1)
            weight_low(2)
            dve.wait_ge(tables_in, 2 * 16)
            for table, m in ((dq, 0), (dk, 1)):
                for g in range(KC):
                    ins = dve.tensor_scalar(table[:, g, :], table[:, g, :], unscale[:, m, g:g + 1], 1.0 / NORM,
                                            ALU.mult, ALU.mult)
            ins.then_inc(tables_ok, 1)
            dve.wait_ge(tables_ok, 1)
            steps(dve, step)

        @block.scalar
        def _(act):
            def copy_xh(s, kc):
                act.wait_ge(xnT_ps, s.count(2, kc + 1))
                act.copy(xh[:, kc, :], ps[:, xn_bank(s, kc), :]).then_inc(xh_sb, 1)

            def copy_v(s, half):
                act.wait_ge(v_ps, s.count(2, half + 1))
                act.copy(v[:, 2 * half:2 * half + 2, :],
                         ps[:, (MISC, STATE)[half], :].rearrange("p (j c) -> p j c", j=2)).then_inc(v_sb, 1)

            def store(s):
                act.wait_ge(res_ok, s.count(2, 2 + FREE))
                act.dma_start(out_v[s.count(1)], res[s.parity][:, :, :]).then_inc(stored[s.parity], 16)

            def finish_last():
                act.wait_ge(gn_st, LAST.count(GN_STEPS, GN_STEPS))
                for half in range(2):
                    act.activation(yn[:, 0, tokens(half)], ps[:, Y, tokens(half)], ACT.Identity, bias=gbias[:, 0:1],
                                   scale=gscale[:, 0:1]).then_inc(yn_sb, 1)
                    act.wait_ge(yn_sb, LAST.count(2, half + 1))
                    act.copy(yh[:, 0, tokens(half)], yn[:, 0, tokens(half)]).then_inc(yh_sb, 1)
                store(LAST + -1)
                for t in range(NT):
                    act.wait_ge(xn2T_ps, LAST.count(2, t + 1 + FREE))
                    act.copy(hi[:, :, t * P:(t + 1) * P],
                             ps[:, LAST_XN2T[t], 0:D].rearrange("p (k t) -> p k t", k=KC)).then_inc(hi_sb, 1)

            def step(cur, has_cur, last=False):
                has_prev = not cur.is_(0)
                prev = cur + -1
                if not has_cur:
                    return finish_last()
                if has_prev:
                    act.wait_ge(gn_st, prev.count(GN_STEPS, GN_STEPS))
                    for g in range(KC):
                        act.activation(yn[:, g, :], ps[:, Y + g, :], ACT.Identity, bias=gbias[:, g:g + 1],
                                       scale=gscale[:, g:g + 1]).then_inc(yn_sb, 1)
                    for g in range(KC):
                        act.wait_ge(yn_sb, prev.count(2, g + 1))
                        act.copy(yh[:, g, :], yn[:, g, :]).then_inc(yh_sb, 1)
                copy_v(cur, 0)
                if has_prev:
                    copy_v(cur, 1)
                for half in range(2):
                    act.wait_ge(ktok_ps, cur.count(2, half + 1))
                    act.copy(ktok[:, 2 * half:2 * half + 2, :],
                             ps[:, 2 + half, :].rearrange("p (j c) -> p j c", j=2)).then_inc(ktok_sb, 1)
                if not has_prev:
                    copy_v(cur, 1)
                act.wait_ge(x_in[cur.parity], cur.same_parity_count(16, 16))
                act.copy(x1[cur.parity][:, :, :], xs[cur.parity][:, :, :]).then_inc(x_copied, 1)
                if cur.is_(0):
                    act.wait_ge(w_in, N_W)
                    act.wait_ge(wo_factor_ok, 1)
                    act.activation(wo16[:, 0, :, :], wo[:, :, :], ACT.Identity, scale=wo_factor[:, :]).then_inc(wo_hi, 1)
                if has_prev:
                    act.wait_ge(nb2_ok, prev.count(1, 1))
                    if not prev.is_(0):
                        act.wait_ge(xn2T_ps, prev.count(2, FREE))
                    for j in range(NT // 2, NT):
                        ins = act.activation(xn2[:, j, :], x1[prev.parity][:, j, :], ACT.Identity,
                                             bias=nb2[:, j:j + 1], scale=rs2[:, j:j + 1])
                    ins.then_inc(xn2b_ok, 1)
                    for kc in range(KC):
                        act.wait_ge(xn2T_ps, prev.count(2, kc + 1 + FREE))
                        act.copy(hi[:, kc, :], ps[:, MISC, :]).then_inc(hi_sb, 1)
                if not last:
                    for kc in range(KC):
                        copy_xh(cur + 1, kc)
                if has_prev and not last:
                    store(prev)

            def weight_high(m):
                act.wait_ge(rowinv_ok, m + 1)
                for g in range(KC):
                    ins = act.activation(w16[m][:, 0, g, :], wn[m][:, g, :], ACT.Identity, scale=rowinv[:, m, g:g + 1])
                ins.then_inc(w16_hi, 1)

            def copy_wT(m):
                act.wait_ge(wT_ps, m + 1)
                act.copy(w16T[m][:, :, :, :].rearrange("p h k d -> p (h k d)"),
                         ps[:, Y + m % 2, :].bitcast(F16)).then_inc(wT_sb, 1)

            weight_high(0)
            weight_high(1)
            copy_xh(Seq(0), 0)
            copy_xh(Seq(0), 1)
            copy_wT(0)
            weight_high(2)
            copy_wT(1)
            copy_wT(2)
            steps(act, step)

        @block.gpsimd
        def _(pool):
            pool.memset(neg_half[:, :], -0.5).then_inc(const_ok, 1)
            for done in (res_ok, xn2_ok, xn2T_ps, ffn_sb, *stored):
                pool.sem_inc(done, FREE)
            pool.wait_ge(const_ok, 1)

            def norm1(s):
                pool.wait_ge(ln1_st, s.count(2, 2))
                pool.tensor_tensor(rs1[:, :], ve1[:, :], neg_half[:, :], ALU.pow).then_inc(rs1_ok, 1)
                if s.is_(0):
                    return
                pool.wait_ge(rs1_ok, s.count(1, 1))
                pool.wait_ge(xnT_ps, s.count(2))
                pool.tensor_tensor(pool_gate[:, :], neg_half[:, 0:1], neg_half[:, 0:1], ALU.add)
                for j in range(NT):
                    ins = pool.tensor_scalar(xn[:, j, :], xs[s.parity][:, j, :], nm1[:, j:j + 1], rs1[:, j:j + 1],
                                             ALU.add, ALU.mult)
                ins.then_inc(xn_ok, 1)

            def norm2(s):
                pool.wait_ge(ln2_st, s.count(2, 2))
                pool.tensor_tensor(rs2[:, :], ve2[:, :], neg_half[:, :], ALU.pow).then_inc(rs2_ok, 1)
                pool.wait_ge(rs2_ok, s.count(1, 1))
                if not s.is_(0):
                    pool.wait_ge(xn2T_ps, s.count(2, FREE))
                pool.tensor_tensor(nb2[:, :], nm2[:, :], rs2[:, :], ALU.mult).then_inc(nb2_ok, 1)
                for j in range(NT // 2):
                    ins = pool.tensor_scalar(xn2[:, j, :], x1[s.parity][:, j, :], nm2[:, j:j + 1], rs2[:, j:j + 1],
                                             ALU.add, ALU.mult)
                ins.then_inc(xn2_ok, 1)

            def add_bias(s, half):
                pool.wait_ge(ffn_sb, s.count(2, half + 1 + FREE))
                j = slice(2 * half, 2 * half + 2)
                pool.tensor_tensor(f[:, j, :], f[:, j, :], by_tile(1), ALU.add).then_inc(bias_ok, 1)

            def head_rsqrt(s):
                pool.wait_ge(gn_st, s.count(GN_STEPS, GN_VARIANCE))
                pool.tensor_tensor(grs[:, :], gve[:, :], neg_half[:, 0:KC], ALU.pow).then_inc(grs_ok, 1)

            def step(cur, has_cur, last=False):
                has_prev = not cur.is_(0)
                prev = cur + -1
                if not last:
                    norm1(cur + 1)
                if not has_cur:
                    for t in range(NT):
                        pool.wait_ge(ln2_st, LAST.count(2, 2 * t + 2))
                        pool.tensor_tensor(rs2[:, t:t + 1], ve2[:, t:t + 1], neg_half[:, t:t + 1],
                                           ALU.pow).then_inc(rs2_ok, 1)
                    return
                if has_prev:
                    norm2(prev)
                    add_bias(prev, 0)
                    if last:
                        head_rsqrt(cur)
                    add_bias(prev, 1)
                    add_x1(pool, prev, 0)
                if not last:
                    head_rsqrt(cur)

            norm1(Seq(0))
            pool.wait_ge(reach_ok, 1)
            pool.partition_all_reduce(reach_all[:, :], reach[:, 0:2], P, bass.bass_isa.ReduceOp.max).then_inc(reach_max, 1)
            steps(pool, step)


def constants():
    start, stop = np.log(1.0 / 32.0), np.log(1.0 / 512.0)
    ramp = np.linspace(start, stop, H).astype(np.float32)
    gamma = (np.float32(1.0) - np.exp(ramp)).astype(np.float64)
    power = np.arange(L) - L // 2
    by_head = gamma[:, None] ** power[None, :]
    decay_q = np.repeat(by_head, DH, axis=0).astype(np.float32)
    decay_k = np.repeat(1.0 / by_head, DH, axis=0).astype(np.float32)
    n = np.arange(P)
    same = (n[:, None] // DH) == (n[None, :] // DH)
    squares = np.stack([np.eye(P), n[:, None] <= n[None, :], same, same / DH]).astype(np.float32)
    return decay_q, decay_k, squares


def by_partition(vectors):
    return np.stack(vectors).reshape(len(vectors), KC, P).transpose(2, 0, 1)


def kernel(**inputs):
    import numpy as _np
    import concourse.bacc as _bacc
    from concourse import mybir as _mybir
    from concourse.bass_utils import run_bass_kernel_spmd as _run

    nc = _bacc.Bacc("TRN2", target_bir_lowering=False, num_devices=1)
    a = {k: _np.asarray(v) for k, v in inputs.items()}
    decay_q, decay_k, squares = constants()
    given = {
        "x": a["L0_attn_x"],
        "wq": a["L0_attn_Wq"], "wk": a["L0_attn_Wk"], "wv": a["L0_attn_Wv"],
        "wo_t": a["L0_attn_Wo"].T, "ffn_t": a["L0_ffn_weights"].T,
        "columns": by_partition([a["L0_attn_gn_weight"], a["L0_attn_gn_bias"]]),
        "ffn_rows": _np.broadcast_to(_np.stack([a["L0_ffn_scale"], a["L0_ffn_bias"]]), (P, 2, D)),
        "decay_q": decay_q, "decay_k": decay_k, "squares": squares,
    }
    given = {k: _np.ascontiguousarray(v) for k, v in given.items()}
    aps = [nc.dram_tensor(k, v.shape, _mybir.dt.from_np(v.dtype), kind="ExternalInput").ap() for k, v in given.items()]
    res = nc.dram_tensor("res_out", given["x"].shape, _mybir.dt.from_np(given["x"].dtype), kind="ExternalOutput").ap()
    build(nc, *aps, res)
    r = _run(nc, [given], core_ids=[0])
    return r.results[0]["res_out"]
```
